# Optimizing a Trainium2 kernel written in Bass

```python
import numpy as np
import jax
import jax.numpy as jnp

def _softmax(x, axis=-1):
    return jax.nn.softmax(x, axis=axis)

def _gelu(x):
    return jax.nn.gelu(x, approximate=True)

def _silu(x):
    return jax.nn.silu(x)

def _sigmoid(x):
    return jax.nn.sigmoid(x)

def _layernorm(x, axis=-1, eps=1e-05):
    m = jnp.mean(x, axis=axis, keepdims=True)
    v = jnp.var(x, axis=axis, keepdims=True)
    return (x - m) / jnp.sqrt(v + eps)

def _scatter_add(tgt, idx, src, axis=0):
    return tgt.at[idx].add(src)

def _segment_sum(src, seg, n):
    return jax.ops.segment_sum(src, seg, n)
kernel_name = 'mk_audio_tower_d1_tok_audfeat512_r4_ddf76b'

def setup_inputs(seed: int=0):
    np.random.seed(seed)
    _w = jnp.asarray

    def _rec_inputs():
        import jax
        import jax.numpy as jnp
        _rk = jax.random.key(seed)
        x = -0.00042137 + 0.99996 * jax.random.normal(jax.random.fold_in(_rk, 1), (128, 750, 64), jnp.float32)
        return x
    x = _rec_inputs()

    def _L0_tok_setup():
        import jax, jax.numpy as jnp
        import numpy as np
        import math
        B, L, C_IN = (64, 792, 64)
        D_MODEL, K = (128, 16)
        W = L // K

        def _positional(S, d, dtype):
            pos = jnp.arange(S, dtype=jnp.float32)[:, None]
            div = jnp.exp(jnp.arange(0, d, 2, dtype=jnp.float32) * (-math.log(10000.0) / d))
            pe = jnp.zeros((S, d), jnp.float32)
            pe = pe.at[:, 0::2].set(jnp.sin(pos * div))
            pe = pe.at[:, 1::2].set(jnp.cos(pos * div))
            return pe.astype(dtype)

        def _gather_cols(xt, idx, L_):
            b, c = (xt.shape[0], xt.shape[1])
            valid = (idx >= 0) & (idx < L_)
            idxc = jnp.clip(idx, 0, L_ - 1).reshape(b, 1, -1)
            g = jnp.take_along_axis(xt, jnp.broadcast_to(idxc, (b, c, idxc.shape[-1])), axis=2)
            g = g.reshape(b, c, idx.shape[1], idx.shape[2])
            return jnp.where(valid[:, None], g, 0.0)
        key = jax.random.key(seed)
        ks = jax.random.split(key, 6)
        fan_in = C_IN * K
        std = math.sqrt(2.0 / (1 + 0.01 ** 2) / fan_in)
        return {'x': jax.random.normal(ks[0], (B, L, C_IN), jnp.float32), 'w_off': jax.random.normal(ks[1], (2 * K, C_IN, K), jnp.float32) * std, 'b_off': jax.random.normal(ks[2], (2 * K,), jnp.float32) * 0.02, 'w_def': jax.random.normal(ks[3], (D_MODEL, C_IN, K), jnp.float32) * std, 'b_def': jax.random.normal(ks[4], (D_MODEL,), jnp.float32) * 0.02, 'cls_token': jax.random.normal(ks[5], (1, 1, D_MODEL), jnp.float32)}
    _L0_tok_all = _L0_tok_setup()
    _L0_tok_in = {k: v for k, v in _L0_tok_all.items() if k in ('w_off', 'b_off', 'w_def', 'b_def', 'cls_token')}
    del _L0_tok_all

    def _L0_attn_setup():
        import jax, jax.numpy as jnp
        import numpy as np
        B, S, E, H = (4, 256, 128, 16)
        key = jax.random.key(seed)
        ks = jax.random.split(key, 6)
        return {'x': jax.random.normal(ks[0], (B, S, E), dtype=jnp.float32), 'Wq': jax.random.normal(ks[1], (E, E), dtype=jnp.float32) * E ** (-0.5), 'Wk': jax.random.normal(ks[2], (E, E), dtype=jnp.float32) * E ** (-0.5), 'Wv': jax.random.normal(ks[3], (E, E), dtype=jnp.float32) * E ** (-0.5), 'W1': jax.random.normal(ks[4], (H, 2 * E), dtype=jnp.float32) * (2 * E) ** (-0.5), 'b1': jnp.zeros((H,), dtype=jnp.float32), 'W2': jax.random.normal(ks[5], (1, H), dtype=jnp.float32) * H ** (-0.5), 'b2': jnp.zeros((1,), dtype=jnp.float32)}
    _L0_attn_all = _L0_attn_setup()
    _L0_attn_in = {k: v for k, v in _L0_attn_all.items() if k in ('Wq', 'Wk', 'Wv', 'W1', 'b1', 'W2', 'b2')}
    del _L0_attn_all

    def _L0_ffn_setup():
        import jax, jax.numpy as jnp
        import numpy as np
        B, S, H, E, K, DF, SH = (8, 1024, 128, 8, 2, 128, 128)
        key = jax.random.key(seed)
        ks = jax.random.split(key, 10)
        n = lambda i, shape, sc: jax.random.normal(ks[i], shape, jnp.float32) * sc
        return {'hidden_states': n(0, (B, S, H), 1.0), 'gate_w': n(1, (E, H), 0.05), 'w1': n(2, (E, H, DF), 0.05), 'b1': n(3, (E, DF), 0.01), 'w2': n(4, (E, DF, H), 0.05), 'b2': n(5, (E, H), 0.01), 'sw1': n(6, (H, SH), 0.05), 'sb1': n(7, (SH,), 0.01), 'sw2': n(8, (SH, H), 0.05), 'sb2': n(9, (H,), 0.01)}
    _L0_ffn_all = _L0_ffn_setup()
    _L0_ffn_in = {k: v for k, v in _L0_ffn_all.items() if k in ('gate_w', 'w1', 'b1', 'w2', 'b2', 'sw1', 'sb1', 'sw2', 'sb2')}
    del _L0_ffn_all
    return {'x': x, 'L0_tok_w_off': _L0_tok_in['w_off'], 'L0_tok_b_off': _L0_tok_in['b_off'], 'L0_tok_w_def': _L0_tok_in['w_def'], 'L0_tok_b_def': _L0_tok_in['b_def'], 'L0_tok_cls_token': _L0_tok_in['cls_token'], 'L0_attn_Wq': _L0_attn_in['Wq'], 'L0_attn_Wk': _L0_attn_in['Wk'], 'L0_attn_Wv': _L0_attn_in['Wv'], 'L0_attn_W1': _L0_attn_in['W1'], 'L0_attn_b1': _L0_attn_in['b1'], 'L0_attn_W2': _L0_attn_in['W2'], 'L0_attn_b2': _L0_attn_in['b2'], 'L0_ffn_gate_w': _L0_ffn_in['gate_w'], 'L0_ffn_w1': _L0_ffn_in['w1'], 'L0_ffn_b1': _L0_ffn_in['b1'], 'L0_ffn_w2': _L0_ffn_in['w2'], 'L0_ffn_b2': _L0_ffn_in['b2'], 'L0_ffn_sw1': _L0_ffn_in['sw1'], 'L0_ffn_sb1': _L0_ffn_in['sb1'], 'L0_ffn_sw2': _L0_ffn_in['sw2'], 'L0_ffn_sb2': _L0_ffn_in['sb2']}

def reference(x, L0_tok_w_off, L0_tok_b_off, L0_tok_w_def, L0_tok_b_def, L0_tok_cls_token, L0_attn_Wq, L0_attn_Wk, L0_attn_Wv, L0_attn_W1, L0_attn_b1, L0_attn_W2, L0_attn_b2, L0_ffn_gate_w, L0_ffn_w1, L0_ffn_b1, L0_ffn_w2, L0_ffn_b2, L0_ffn_sw1, L0_ffn_sb1, L0_ffn_sw2, L0_ffn_sb2):
    import jax
    import jax.numpy as jnp

    def _L0_tok_ref(x, w_off, b_off, w_def, b_def, cls_token):
        import jax, jax.numpy as jnp
        import numpy as np
        import math
        B, L, C_IN = (64, 792, 64)
        D_MODEL, K = (128, 16)
        W = L // K

        def _positional(S, d, dtype):
            pos = jnp.arange(S, dtype=jnp.float32)[:, None]
            div = jnp.exp(jnp.arange(0, d, 2, dtype=jnp.float32) * (-math.log(10000.0) / d))
            pe = jnp.zeros((S, d), jnp.float32)
            pe = pe.at[:, 0::2].set(jnp.sin(pos * div))
            pe = pe.at[:, 1::2].set(jnp.cos(pos * div))
            return pe.astype(dtype)

        def _gather_cols(xt, idx, L_):
            b, c = (xt.shape[0], xt.shape[1])
            valid = (idx >= 0) & (idx < L_)
            idxc = jnp.clip(idx, 0, L_ - 1).reshape(b, 1, -1)
            g = jnp.take_along_axis(xt, jnp.broadcast_to(idxc, (b, c, idxc.shape[-1])), axis=2)
            g = g.reshape(b, c, idx.shape[1], idx.shape[2])
            return jnp.where(valid[:, None], g, 0.0)
        b, l, c = x.shape
        w = l // K
        xr = x[:, :w * K, :].reshape(b, w, K, c)
        off = jnp.einsum('bwkc,ock->bow', xr, w_off) + b_off[None, :, None]
        dy = off[:, 0::2]
        dx = off[:, 1::2]
        base = (jnp.arange(w)[None, :] * K + jnp.arange(K)[:, None]).astype(x.dtype)
        px = base[None] + dx
        x0 = jnp.floor(px)
        frac = px - x0
        x0i = x0.astype(jnp.int32)
        xt = x.transpose(0, 2, 1)
        v0 = _gather_cols(xt, x0i, l)
        v1 = _gather_cols(xt, x0i + 1, l)
        wy = jnp.maximum(0.0, 1.0 - jnp.abs(dy))
        val = wy[:, None] * ((1.0 - frac)[:, None] * v0 + frac[:, None] * v1)
        out = jnp.einsum('bckw,dck->bwd', val, w_def) + b_def
        tok = jnp.concatenate([jnp.broadcast_to(cls_token, (b, 1, D_MODEL)), out], axis=1)
        pe = _positional(w + 1, D_MODEL, tok.dtype)
        return tok + pe[None]

    def _L0_attn_ref(x, Wq, Wk, Wv, W1, b1, W2, b2):
        import jax, jax.numpy as jnp
        import numpy as np
        B, S, E, H = (4, 256, 128, 16)
        embed_dim = x.shape[-1]
        Q = jnp.einsum('bse,oe->bso', x, Wq)
        K = jnp.einsum('bse,oe->bso', x, Wk)
        V = jnp.einsum('bse,oe->bso', x, Wv)
        scores = jnp.einsum('bqe,bke->bqk', Q, K) / jnp.sqrt(jnp.float32(embed_dim))
        W1q, W1k = (W1[:, :embed_dim], W1[:, embed_dim:])
        hq = jnp.einsum('bqe,he->bqh', Q, W1q)
        hk = jnp.einsum('bke,he->bkh', K, W1k)
        hid = jnp.tanh(hq[:, :, None, :] + hk[:, None, :, :] + b1)
        est = jnp.einsum('bqkh,h->bqk', hid, W2[0]) + b2[0]
        attn = jax.nn.softmax(scores + est, axis=-1)
        return jnp.einsum('bqk,bke->bqe', attn, V)

    def _L0_ffn_ref(hidden_states, gate_w, w1, b1, w2, b2, sw1, sb1, sw2, sb2):
        import jax, jax.numpy as jnp
        import numpy as np
        B, S, H, E, K, DF, SH = (8, 1024, 128, 8, 2, 128, 128)
        x = hidden_states
        xf = x.reshape(-1, x.shape[-1])
        T = xf.shape[0]
        scores = jax.nn.softmax(xf @ gate_w.T, axis=-1)
        topk_w, topk_i = jax.lax.top_k(scores, K)
        topk_w = topk_w / (topk_w.sum(-1, keepdims=True) + 1e-20)
        combine = jnp.zeros((T, E), xf.dtype).at[jnp.arange(T)[:, None], topk_i].add(topk_w)
        h1 = jax.nn.relu(jnp.einsum('th,ehf->tef', xf, w1) + b1)
        eo = jnp.einsum('tef,efh->teh', h1, w2) + b2
        y = jnp.einsum('te,teh->th', combine, eo)
        shared = jax.nn.relu(xf @ sw1 + sb1) @ sw2 + sb2
        return (y + shared).reshape(x.shape)
    h = _L0_tok_ref(x, L0_tok_w_off, L0_tok_b_off, L0_tok_w_def, L0_tok_b_def, L0_tok_cls_token)
    h = h + _L0_attn_ref(_layernorm(h, axis=-1), L0_attn_Wq, L0_attn_Wk, L0_attn_Wv, L0_attn_W1, L0_attn_b1, L0_attn_W2, L0_attn_b2)
    h = h + _L0_ffn_ref(_layernorm(h, axis=-1), L0_ffn_gate_w, L0_ffn_w1, L0_ffn_b1, L0_ffn_w2, L0_ffn_b2, L0_ffn_sw1, L0_ffn_sb1, L0_ffn_sw2, L0_ffn_sb2)
    return h

_drawn_inputs = setup_inputs


def setup_inputs(seed=0):
    import zlib

    import numpy as np

    out = dict(_drawn_inputs(seed))
    spreads = {'L0_attn_b1': (0.0, 0.8)}
    factors = {'L0_ffn_b1': 21.913, 'L0_ffn_b2': 8.0, 'L0_ffn_sb1': 8.0, 'L0_ffn_sb2': 5.523}
    for name, (base, spread) in spreads.items():
        noise = np.random.default_rng([zlib.crc32(name.encode()), seed]).standard_normal(out[name].shape)
        drawn = base * np.exp(spread * noise) if base else spread * noise
        out[name] = jnp.asarray(drawn.astype(out[name].dtype))
    for name, factor in factors.items():
        out[name] = (out[name] * factor).astype(out[name].dtype)
    return out
```

```python
import concourse.bass as bass
from concourse import mybir
from contextlib import ExitStack

B, L, C = 128, 750, 64
K = 16
W = L // K
D = 128
S = W + 1
NB = 8
UNITS = B // NB
WT = [16, 16, 14]
W0 = [0, 16, 32]
NT = [NB * w for w in WT]
T0 = [0, 128, 256]
TOK = NB * W
COLS = NB * S
KP = K // 2
H = 16
E = 8
RT = 94
RN = COLS // RT
QG = 12
EPS = 1e-5
ROUND = 8388608.0

CONSTS = [
    ("ident", [128, 128]), ("wof", [128, KP * 32]), ("stk", [128, 32]), ("boff", [128, 32]),
    ("base", [128, 3 * K]), ("rowbase", [128, 3]), ("wdef", [128, KP * D]), ("bdef", [128, 1]), ("cls", [128, 1]),
    ("peT", [128, S]), ("center", [128, 128]), ("wq", [128, 128]), ("wk", [128, 128]), ("wvT", [128, 128]),
    ("w1qT", [128, H]), ("w1kT", [128, H]), ("b1h", [128, 1]), ("gwT", [128, E]), ("tri", [128, E * E]),
    ("w1e", [128, 9 * 128]), ("w2e", [128, 9 * 128]), ("fb1", [128, 9]), ("sel", [24, E * 128]), ("b2col", [128, 1]),
]
ROWS = [("w2col", [H, 1]), ("b2e", [9, 128])]


def wait(eng, sem, n):
    if isinstance(n, int) and n <= 0:
        return
    eng.wait_ge(sem, n)


class Chain:

    def __init__(self, eng, sem):
        self.eng, self.sem, self.base, self.n = eng, sem, 0, 0

    def __call__(self, ins):
        ins.then_inc(self.sem, 1)
        self.n += 1
        self.eng.wait_ge(self.sem, self.base + self.n)

    def mark(self):
        self.at = self.n

    def loop(self, i, first, per):
        self.outer = self.base + self.n
        self.base, self.n = self.outer + (i - first) * per, 0

    def end(self, trips, per):
        assert self.n == per, (self.n, per)
        self.base, self.n = self.outer + trips * per, 0


def audio_tower(nc, x, consts, rows, out):
    fp32, bf16, i32 = mybir.dt.float32, mybir.dt.bfloat16, mybir.dt.int32
    ALU, ACT, AX = mybir.AluOpType, mybir.ActivationFunctionType, mybir.AxisListType

    turned = nc.dram_tensor("turned", (NB, S * S), fp32, kind="Internal").ap()
    ctx = ExitStack()
    with ctx:
        def sb(name, shape, dt=fp32):
            return ctx.enter_context(nc.sbuf_tensor(name, shape, dt))

        def sem(name):
            return ctx.enter_context(nc.semaphore(name))

        cs = {name: sb("c_" + name, shape) for name, shape in CONSTS}
        ident, center = cs["ident"], cs["center"]
        wof = cs["wof"][:, :].rearrange("p (k o) -> p k o", o=32)
        wdef = cs["wdef"][:, :].rearrange("p (k d) -> p k d", d=D)
        w1e = cs["w1e"][:, :].rearrange("p (e f) -> p e f", f=128)
        w2e = cs["w2e"][:, :].rearrange("p (e f) -> p e f", f=128)
        base = cs["base"][:, :].rearrange("p (j k) -> p j k", k=K)
        identb = sb("identb", [128, 128], bf16)
        selb = sb("selb", [24, E, 128], bf16)
        ones = sb("ones", [128, 128])
        mean1 = sb("mean1", [128, 1])
        scoreB = sb("scoreB", [128, 128])
        w1pad = sb("w1pad", [128, 2, 2, 32])
        w2blk = sb("w2blk", [128, NB])
        b2pad = sb("b2pad", [128, 128])
        pe_b = sb("pe_b", [128, S])
        cls_pe = sb("cls_pe", [128, 1])

        xt = [sb(f"xt{p}", [128, 3, K * C]) for p in range(2)]
        XT = sb("XT", [128, KP, TOK])
        off4 = sb("off4", [128, TOK])
        offs = sb("offs", [128, 3, 32])
        px = sb("px", [128, 3, K])
        nwy = sb("nwy", [128, 3, K])
        rr = sb("rr", [128, 3, K])
        e01 = sb("e01", [128, 3, K, 2])
        e01f = e01[:, :, :, :].rearrange("p j k s -> p (j k s)")
        rowb = sb("rowb", [128, 3])
        idx = [sb(f"idx{p}", [128, 3 * K], i32) for p in range(2)]
        aw = [sb(f"aw{p}", [128, 3, K, 2]) for p in range(2)]
        G = [sb(f"G{p}", [128, 3, K, 2 * C]) for p in range(2)]
        VAL = sb("VAL", [128, 3, K * C])
        VT = sb("VT", [128, KP, TOK])
        h0 = sb("h0", [128, NB, S])
        SQ = sb("SQ", [128, COLS])
        HC = sb("HC", [128, COLS])
        Z = sb("Z", [128, NB, S])
        Zf = Z[:, :, :].rearrange("p b s -> p (b s)")
        var = sb("var", [RT, RN])
        nt_ = sb("nt_", [RT, RN])
        ry = sb("ry", [RT, RN])
        ishift = sb("ishift", [RT, RN], i32)
        diag = sb("diag", [RT, RN, RT])
        Y = sb("Y", [128, NB, S])
        V = sb("V", [128, NB, 128])
        hq = sb("hq", [128, S])
        hk = sb("hk", [128, S])
        TH = sb("TH", [128, S, S])
        est = sb("est", [128, 2, QG // 2 * S])
        estq = sb("estq", [S, NB, S])
        SC = sb("SC", [S, NB, S])
        smx = sb("smx", [S, NB])
        ssum = sb("ssum", [S, NB])
        sinv = sb("sinv", [S, NB])
        PR = sb("PR", [S, NB, S])
        PT = sb("PT", [128, COLS])
        h1 = sb("h1", [128, COLS])
        lg = sb("lg", [RT, RN, E])
        gmx = sb("gmx", [RT, RN])
        gp = sb("gp", [RT, RN, E])
        gsum = sb("gsum", [RT, RN])
        ginv = sb("ginv", [RT, RN])
        gt = sb("gt", [RT, RN, E, E])
        eq = sb("eq", [RT, RN, E, E])
        rank = sb("rank", [RT, RN, E])
        c9 = sb("c9", [RT, RN, 9])
        c3 = sb("c3", [RT, RN, 3, E], bf16)
        cres = sb("cres", [RT, RN, E])
        cT3 = sb("cT3", [24, COLS], bf16)
        cT9 = sb("cT9", [128, COLS])
        HE = [sb(f"HE{i}", [128, COLS]) for i in range(2)]
        GE = [sb(f"GE{i}", [128, COLS]) for i in range(2)]
        h2 = sb("h2", [128, COLS])
        OUTS = [sb(f"OUTS{p}", [RT, RN, 128]) for p in range(2)]

        bank = [ctx.enter_context(nc.psum_tensor(f"bank{i}", [128, 512], fp32)) for i in range(8)]

        bank2b = bank[2][:, :].bitcast(bf16)

        def cols(t):
            return bank[t][:, 0:COLS]

        const_in, zeroed, psum_zeroed, setup_psum, setup_mats, dve_consts = (
            sem(n) for n in ("const_in", "zeroed", "psum_zeroed", "setup_psum", "setup_mats", "dve_consts"))
        blk_in = sem("blk_in")
        NCONST = 16 * len(CONSTS)
        x_in = [[sem(f"x_in{p}{j}") for j in range(3)] for p in range(2)]
        gathered = [[sem(f"gathered{p}{j}") for j in range(3)] for p in range(2)]
        out_done = [sem(f"out_done{p}") for p in range(2)]
        est_out, est_moved = sem("est_out"), sem("est_moved")
        tp_full = sem("tp_full")
        xt_ready, vt_ready = sem("xt_ready"), sem("vt_ready")
        off4_full, off4_ready, ot_full, ot_read, idx_ready = (
            sem(n) for n in ("off4_full", "off4_ready", "ot_full", "ot_read", "idx_ready"))
        val_ready, tok_full, h0_ready = (sem(n) for n in ("val_ready", "tok_full", "h0_ready"))
        hc_full, sq_ready, hc_ready, var_full, diag_ready, rstd_full, z_ready = (
            sem(n) for n in ("hc_full", "sq_ready", "hc_ready", "var_full", "diag_ready", "rstd_full", "z_ready"))
        hqk_full, y_full, y_ready, v_full, v_ready, add_ready, th_ready = (
            sem(n) for n in ("hqk_full", "y_full", "y_ready", "v_full", "v_ready", "add_ready", "th_ready"))
        s_full, est_full, est_ready, sc_ready, exp_ready, p_ready, pt_full, pt_ready, av_full, h1_ready = (
            sem(n) for n in ("s_full", "est_full", "est_ready", "sc_ready", "exp_ready", "p_ready", "pt_full",
                             "pt_ready", "av_full", "h1_ready"))
        gl_full, lg_ready, gexp_ready, c_ready, ct_full, ct_ready = (
            sem(n) for n in ("gl_full", "lg_ready", "gexp_ready", "c_ready", "ct_full", "ct_ready"))
        up_full, he_ready, cb_full, ge_ready, down_done, yacc_full, h2_ready, out_full, outs_ready = (
            sem(n) for n in ("up_full", "he_ready", "cb_full", "ge_ready", "down_done", "yacc_full", "h2_ready",
                             "out_full", "outs_ready"))
        passed = sem("passed")
        dve_chain, act_chain = sem("dve_chain"), sem("act_chain")

        def groups_x(m, h):
            return 6 * h if isinstance(m, int) and m == 0 else 12 * (2 * m + h) - 6

        def groups_v(u):
            if isinstance(u, int) and u == UNITS - 1:
                return 12 * u + 6
            return 12 * u + 12

        block = ctx.enter_context(nc.Block())

        def steps(eng, step, chain=None, last=UNITS):
            if chain:
                chain.mark()
            for h in range(2):
                step(0, h)
            per = chain.n - chain.at if chain else 0
            trips = last // 2 - 1
            with eng.Fori(1, last // 2) as i:
                if chain:
                    chain.loop(i, 1, per)
                for h in range(2):
                    step(i, h)
            if chain:
                chain.end(trips, per)
            for m in range(last // 2, UNITS // 2):
                for h in range(2):
                    step(m, h)

        @block.sync
        def _(sp):
            def load_x(m, h):
                u = 2 * m + h
                for j in range(3):
                    if not (isinstance(m, int) and m == 0):
                        sp.wait_ge(tp_full, groups_x(m - 1, h) + 2 * (j + 1))
                    src = x[bass.ds(NB * u, NB), W0[j] * K * C:(W0[j] + WT[j]) * K * C]
                    sp.dma_start(xt[h][0:NT[j], j, :],
                                 src.rearrange("b (w n) -> w b n", w=WT[j])).then_inc(x_in[h][j], 16)

            def step(m, h):
                u = 2 * m + h
                m3, h3 = m + 1 + (h + 1) // 2, (h + 1) % 2
                if not (isinstance(m, int) and 2 * m3 + h3 >= UNITS):
                    load_x(m3, h3)
                sp.wait_ge(est_ready, 2 * (u + 1))
                for g in range(4):
                    n = min(QG, S - QG * g)
                    src = est[32 * g:32 * g + NB, :, :].rearrange("b s n -> b (s n)")[:, 0:n * S]
                    sp.dma_start(turned[:, QG * S * g:QG * S * g + n * S], src).then_inc(est_out, 16)
                sp.wait_ge(est_out, 64 * (u + 1))
                sp.dma_start(estq[:, :, :], turned.rearrange("b (q k) -> q b k", k=S)).then_inc(est_moved, 16)
                sp.wait_ge(outs_ready, u + 1)
                sp.dma_start(out[bass.ds(COLS * u, COLS), :].rearrange("(t r) d -> r t d", r=RT),
                             OUTS[h][:, :, :]).then_inc(out_done[h], 16)

            load_x(0, 0)
            load_x(0, 1)
            load_x(1, 0)
            steps(sp, step, last=UNITS - 4)
            for h in range(2):
                sp.wait_ge(out_done[h], 16 * UNITS // 2)

        @block.gpsimd
        def _(pool):
            pool.memset(w2blk[:, :], 0.0).then_inc(zeroed, 1)
            pool.memset(b2pad[:, :], 0.0).then_inc(zeroed, 1)
            pool.memset(w1pad[:, :, :, :], 0.0).then_inc(zeroed, 1)
            pool.memset(PT[:, :], 0.0).then_inc(zeroed, 1)
            pool.memset(V[:, :, :], 0.0).then_inc(zeroed, 1)
            pool.memset(cT9[:, :], 0.0).then_inc(zeroed, 1)
            pool.memset(c9[:, :, :], 1.0).then_inc(zeroed, 1)
            pool.memset(ones[:, :], 1.0).then_inc(zeroed, 1)
            pool.memset(mean1[:, :], 1.0 / D).then_inc(zeroed, 1)

            def gathers(m, h):
                u = 2 * m + h
                pool.wait_ge(idx_ready, u + 1)
                for j in range(3):
                    if not (isinstance(m, int) and m == 0):
                        pool.wait_ge(val_ready, 3 * u - 5 + j)
                    pool.sem_inc(passed, 1)
                    for k in range(K):
                        col = j * K + k
                        pool.indirect_dma_start(
                            out=G[h][0:NT[j], j, k, :], out_offset=None, in_=x.rearrange("b (l c) -> (b l) c", c=C),
                            in_offset=bass.IndirectOffsetOnAxis(ap=idx[h][0:NT[j], col:col + 1], axis=0),
                        ).then_inc(gathered[h][j], 16)

            steps(pool, gathers)

        @block.scalar
        def _(act):
            chain = Chain(act, act_chain)
            for name, _s in CONSTS:
                act.dma_start(cs[name][:, :], consts[name]).then_inc(const_in, 16)
            act.wait_ge(zeroed, 2)
            for b in range(NB):
                act.dma_start(w2blk[H * b:H * b + H, b:b + 1], rows["w2col"]).then_inc(blk_in, 16)
            act.dma_start(b2pad[0:9, :], rows["b2e"]).then_inc(blk_in, 16)

            def evacuate(first, n, dst, nrow, ready):
                act.wait_ge(tp_full, first + n + 1)
                act.activation(dst, bank[n % 2][:, 0:4 * nrow].rearrange("p (k t) -> p k t", k=4), ACT.Copy).then_inc(ready, 1)

            def stage_a(m, h):
                u = 2 * m + h
                first = groups_x(m, h)
                wait(act, off4_full, u)
                for j in range(3):
                    for half in range(2):
                        evacuate(first, 2 * j + half,
                                 XT[:, 4 * half:4 * half + 4, T0[j]:T0[j] + NT[j]], NT[j], xt_ready)
                wait(act, ot_full, u)
                act.wait_ge(off4_full, u + 1)
                act.activation(off4[:, :], bank[2][:, 0:TOK], ACT.Copy).then_inc(off4_ready, 1)

            def layer_norm(n, b, ready=None):
                act.wait_ge(hc_full, n + 1)
                act.activation(SQ[:, :], cols(b), ACT.Square).then_inc(sq_ready, 1)
                act.activation(HC[:, :], cols(b), ACT.Copy).then_inc(hc_ready, 1)

            def step(m, h):
                u = 2 * m + h
                wait(act, tok_full, u)
                for j in range(3):
                    for half in range(2):
                        evacuate(groups_v(u), 2 * j + half,
                                 VT[:, 4 * half:4 * half + 4, T0[j]:T0[j] + NT[j]], NT[j], vt_ready)
                if not (isinstance(m, int) and m + 1 >= UNITS // 2):
                    stage_a(m + 1, h)
                layer_norm(2 * u, 5)
                act.wait_ge(y_full, u + 1)
                act.activation(Y[:, :, :].rearrange("p b s -> p (b s)"), cols(7), ACT.Copy).then_inc(y_ready, 1)
                for half in range(2):
                    act.wait_ge(add_ready, 2 * u + half + 1)
                    q0, q1 = (0, 2 * QG) if half == 0 else (2 * QG, S)
                    act.activation(TH[:, q0:q1, :], TH[:, q0:q1, :], ACT.Tanh).then_inc(th_ready, 1)
                act.wait_ge(v_full, u + 1)
                for half in range(2):
                    act.activation(V[0:S, 4 * half:4 * half + 4, :],
                                   bank[2 + half][0:S, :].rearrange("p (b n) -> p b n", b=4), ACT.Copy).then_inc(v_ready, 1)
                act.wait_ge(sc_ready, u + 1)
                act.activation(SC[:, :, :], SC[:, :, :], ACT.Exp).then_inc(exp_ready, 1)
                act.wait_ge(pt_full, u + 1)
                act.activation(PT[0:S, :], bank[6][0:S, 0:COLS], ACT.Copy).then_inc(pt_ready, 1)
                layer_norm(2 * u + 1, 7)
                act.wait_ge(lg_ready, u + 1)
                act.activation(lg[:, :, :], lg[:, :, :], ACT.Exp).then_inc(gexp_ready, 1)

                def hidden(e):
                    act.wait_ge(up_full, 9 * u + e + 1)
                    if e >= 2:
                        act.wait_ge(ge_ready, 8 * u + e - 1)
                    act.activation(HE[e % 2][:, :], cols(5 + e % 2), ACT.Relu, bias=cs["fb1"][:, e:e + 1]).then_inc(he_ready, 1)

                hidden(0)
                hidden(1)
                act.wait_ge(ct_full, 2 * u + 1)
                act.activation(cT3[:, :], bank2b[0:24, 0:COLS], ACT.Copy).then_inc(ct_ready, 1)
                act.wait_ge(ct_full, 2 * u + 2)
                act.activation(cT9[0:9, :], bank[3][0:9, 0:COLS], ACT.Copy).then_inc(ct_ready, 1)
                for e in range(2, 9):
                    hidden(e)
                act.wait_ge(out_full, u + 1)
                if not (isinstance(m, int) and m == 0):
                    act.wait_ge(out_done[h], 16 * m)
                act.activation(OUTS[h][:, :, :], bank[4][0:RT, :].rearrange("p (t n) -> p t n", t=RN),
                               ACT.Copy).then_inc(outs_ready, 1)

            act.wait_ge(psum_zeroed, 8)
            stage_a(0, 0)
            stage_a(0, 1)
            act.wait_ge(setup_psum, 3)
            act.activation(scoreB[:, :], bank[5][:, 0:128], ACT.Copy, scale=float(D) ** -0.5).then_inc(setup_mats, 1)
            act.wait_ge(zeroed, 9)
            for qk in range(2):
                for par in range(2):
                    act.activation(w1pad[:, qk, par, H * par:H * par + H], bank[6 + qk][:, 0:H], ACT.Copy).then_inc(setup_mats, 1)
            steps(act, step, last=UNITS - 2)

        @block.vector
        def _(dve):
            chain = Chain(dve, dve_chain)
            for b in range(8):
                dve.memset(bank[b][:, :], 0.0).then_inc(psum_zeroed, 1)
            dve.memset(est[:, :, :], 0.0).then_inc(dve_consts, 1)
            dve.wait_ge(const_in, NCONST)
            dve.tensor_copy(identb[:, :], ident[:, :]).then_inc(dve_consts, 1)
            dve.tensor_copy(selb[:, :, :].rearrange("p e n -> p (e n)"), cs["sel"][:, :]).then_inc(dve_consts, 1)
            dve.tensor_copy(rowb[:, :], cs["rowbase"][:, :]).then_inc(dve_consts, 1)
            dve.tensor_scalar(pe_b[:, :], cs["peT"][:, :], cs["bdef"][:, 0:1], None, ALU.add).then_inc(dve_consts, 1)
            dve.tensor_tensor(cls_pe[:, :], cs["cls"][:, :], cs["peT"][:, 0:1], ALU.add).then_inc(dve_consts, 1)
            dve.wait_ge(dve_consts, 6)
            chain(dve.tensor_copy(h0[:, :, 0:1], cls_pe[:, :].unsqueeze(1).broadcast_to([128, NB, 1])))
            dve.wait_ge(psum_zeroed, 8)

            def stage_a(m, h):
                u = 2 * m + h
                dve.wait_ge(ot_full, u + 1)
                dve.tensor_tensor(offs[:, :, :], bank[3][:, 0:96].rearrange("p (j o) -> p j o", o=32),
                                  cs["boff"][:, :].unsqueeze(1).broadcast_to([128, 3, 32]), ALU.add).then_inc(ot_read, 1)
                dve.wait_ge(ot_read, u + 1)
                chain(dve.tensor_tensor(px[:, :, :], offs[:, :, K:2 * K], base, ALU.add))
                chain(dve.scalar_tensor_tensor(nwy[:, :, :], offs[:, :, 0:K], -1.0, offs[:, :, 0:K], ALU.mult, ALU.max))
                chain(dve.tensor_scalar(rr[:, :, :], px[:, :, :], -0.5, 0.0, ALU.add, ALU.max))
                chain(dve.tensor_scalar(nwy[:, :, :], nwy[:, :, :], 1.0, 1.0, ALU.min, ALU.subtract))
                chain(dve.tensor_scalar(rr[:, :, :], rr[:, :, :], float(L - 2), ROUND, ALU.min, ALU.add))
                chain(dve.tensor_scalar(rr[:, :, :], rr[:, :, :], ROUND, None, ALU.subtract))
                chain(dve.tensor_tensor(idx[h][:, :].rearrange("p (j k) -> p j k", k=K), rr[:, :, :],
                                        rowb[:, :].unsqueeze(2).broadcast_to([128, 3, K]), ALU.add))
                chain(dve.tensor_tensor(e01[:, :, :, 0], px[:, :, :], rr[:, :, :], ALU.subtract))
                chain(dve.tensor_scalar(e01[:, :, :, 1], e01[:, :, :, 0], 1.0, None, ALU.subtract))
                chain(dve.scalar_tensor_tensor(e01f, e01f, -1.0, e01f, ALU.mult, ALU.max))
                chain(dve.tensor_scalar(e01f, e01f, 1.0, 1.0, ALU.min, ALU.subtract))
                chain(dve.tensor_scalar(rowb[:, :], rowb[:, :], float(NB * L), None, ALU.add))
                dve.tensor_tensor(aw[h][:, :, :, :], e01[:, :, :, :], nwy[:, :, :].unsqueeze(3).broadcast_to([128, 3, K, 2]),
                                  ALU.mult).then_inc(idx_ready, 1)

            def layer_norm(n, b):
                dve.wait_ge(var_full, n + 1)
                chain(dve.tensor_scalar(var[:, :], bank[6][0:RT, COLS:COLS + RN], EPS, None, ALU.add))
                chain(dve.tensor_scalar(ishift[:, :], var[:, :].bitcast(i32), 1, None, ALU.logical_shift_right))
                chain(dve.tensor_scalar(ry[:, :].bitcast(i32), ishift[:, :], -1.0, float(0x5F3759DF), ALU.mult, ALU.add))
                for _i in range(3):
                    chain(dve.scalar_tensor_tensor(nt_[:, :], ry[:, :], -0.5, ry[:, :], ALU.mult, ALU.mult))
                    chain(dve.tensor_tensor(nt_[:, :], nt_[:, :], var[:, :], ALU.mult))
                    chain(dve.scalar_tensor_tensor(ry[:, :], nt_[:, :], 1.5, ry[:, :], ALU.add, ALU.mult))
                dve.tensor_tensor(diag[:, :, :], ident[0:RT, 0:RT].unsqueeze(1).broadcast_to([RT, RN, RT]),
                                  ry[:, :].unsqueeze(2).broadcast_to([RT, RN, RT]), ALU.mult).then_inc(diag_ready, 1)
                dve.wait_ge(rstd_full, n + 1)
                dve.wait_ge(hc_ready, n + 1)
                dve.tensor_tensor(Zf, HC[:, :], cols(6), ALU.mult).then_inc(z_ready, 1)

            def step(m, h):
                u = 2 * m + h
                for j in range(3):
                    dve.wait_ge(gathered[h][j], 16 * K * (m + 1))
                    g = G[h][0:NT[j], j, :, :].rearrange("p k (s c) -> p (k s) c", s=2)
                    w = aw[h][0:NT[j], j, :, :].rearrange("p k s -> p (k s)").unsqueeze(2).broadcast_to([NT[j], 2 * K, C])
                    chain(dve.tensor_tensor(g, g, w, ALU.mult))
                    if not (isinstance(m, int) and u == 0):
                        dve.wait_ge(tp_full, groups_v(u - 1) + 2 * (j + 1))
                    g = G[h][0:NT[j], j, :, :]
                    dve.tensor_tensor(VAL[0:NT[j], j, :].rearrange("p (k c) -> p k c", c=C), g[:, :, 0:C],
                                      g[:, :, C:2 * C], ALU.add).then_inc(val_ready, 1)
                dve.wait_ge(tok_full, u + 1)
                for j in range(3):
                    s0 = 1 + W0[j]
                    ins = dve.tensor_tensor(
                        h0[:, :, s0:s0 + WT[j]].rearrange("p b s -> p s b"),
                        bank[4][:, T0[j]:T0[j] + NT[j]].rearrange("p (w b) -> p w b", b=NB),
                        pe_b[:, s0:s0 + WT[j]].unsqueeze(2).broadcast_to([128, WT[j], NB]), ALU.add)
                ins.then_inc(h0_ready, 1)
                if not (isinstance(m, int) and m + 1 >= UNITS // 2):
                    stage_a(m + 1, h)
                layer_norm(2 * u, 5)
                dve.wait_ge(hqk_full, u + 1)
                chain(dve.tensor_scalar(hq[:, :], bank[5][:, 0:S], cs["b1h"][:, 0:1], None, ALU.add))
                chain(dve.tensor_copy(hk[:, :], bank[5][:, S:2 * S]))
                for half in range(2):
                    q0, q1 = (0, 2 * QG) if half == 0 else (2 * QG, S)
                    dve.tensor_tensor(TH[:, q0:q1, :], hq[:, q0:q1].unsqueeze(2).broadcast_to([128, q1 - q0, S]),
                                      hk[:, :].unsqueeze(1).broadcast_to([128, q1 - q0, S]), ALU.add).then_inc(add_ready, 1)
                dve.wait_ge(est_full, u + 1)
                for s in range(2):
                    dve.tensor_scalar(est[:, s, :], bank[(5, 7)[s]][:, 0:QG // 2 * S], cs["b2col"][:, 0:1], None,
                                      ALU.add).then_inc(est_ready, 1)
                dve.wait_ge(est_moved, 16 * (u + 1))
                dve.wait_ge(s_full, u + 1)
                chain(dve.tensor_tensor(SC[:, :, :], bank[4][0:S, 0:COLS].rearrange("p (b s) -> p b s", b=NB),
                                        estq[:, :, :], ALU.add))
                chain(dve.reduce_max(smx[:, :], SC[:, :, :], AX.X))
                dve.tensor_tensor(SC[:, :, :], SC[:, :, :], smx[:, :].unsqueeze(2).broadcast_to([S, NB, S]),
                                  ALU.subtract).then_inc(sc_ready, 1)
                dve.wait_ge(exp_ready, u + 1)
                chain(dve.reduce_sum(ssum[:, :], SC[:, :, :], AX.X))
                chain(dve.reciprocal(sinv[:, :], ssum[:, :]))
                dve.tensor_tensor(PR[:, :, :], SC[:, :, :], sinv[:, :].unsqueeze(2).broadcast_to([S, NB, S]),
                                  ALU.mult).then_inc(p_ready, 1)
                dve.wait_ge(av_full, u + 1)
                dve.tensor_tensor(h1[:, :], cols(5), h0[:, :, :].rearrange("p b s -> p (b s)"), ALU.add).then_inc(h1_ready, 1)
                layer_norm(2 * u + 1, 7)
                dve.wait_ge(gl_full, u + 1)
                glv = bank[4][0:RT, 0:RN * E].rearrange("p (t e) -> p t e", e=E)
                chain(dve.reduce_max(gmx[:, :], glv, AX.X))
                dve.tensor_tensor(lg[:, :, :], glv, gmx[:, :].unsqueeze(2).broadcast_to([RT, RN, E]),
                                  ALU.subtract).then_inc(lg_ready, 1)
                dve.wait_ge(gexp_ready, u + 1)
                chain(dve.reduce_sum(gsum[:, :], lg[:, :, :], AX.X))
                chain(dve.reciprocal(ginv[:, :], gsum[:, :]))
                chain(dve.tensor_tensor(gp[:, :, :], lg[:, :, :], ginv[:, :].unsqueeze(2).broadcast_to([RT, RN, E]), ALU.mult))
                other = gp[:, :, :].unsqueeze(2).broadcast_to([RT, RN, E, E])
                own = gp[:, :, :].unsqueeze(3).broadcast_to([RT, RN, E, E])
                chain(dve.tensor_tensor(eq[:, :, :, :], other, own, ALU.is_equal))
                chain(dve.tensor_tensor(eq[:, :, :, :].rearrange("p t i j -> p t (i j)"),
                                        eq[:, :, :, :].rearrange("p t i j -> p t (i j)"),
                                        cs["tri"][0:RT, :].unsqueeze(1).broadcast_to([RT, RN, E * E]), ALU.mult))
                chain(dve.tensor_tensor(gt[:, :, :, :], other, own, ALU.is_gt))
                chain(dve.tensor_tensor(gt[:, :, :, :], gt[:, :, :, :], eq[:, :, :, :], ALU.add))
                chain(dve.reduce_sum(rank[:, :, :], gt[:, :, :, :], AX.X))
                chain(dve.scalar_tensor_tensor(gp[:, :, :], rank[:, :, :], 2.0, gp[:, :, :], ALU.is_lt, ALU.mult))
                chain(dve.reduce_sum(gsum[:, :], gp[:, :, :], AX.X))
                chain(dve.tensor_scalar(gsum[:, :], gsum[:, :], 1e-20, None, ALU.add))
                chain(dve.reciprocal(ginv[:, :], gsum[:, :]))
                chain(dve.tensor_tensor(c9[:, :, 0:E], gp[:, :, :], ginv[:, :].unsqueeze(2).broadcast_to([RT, RN, E]), ALU.mult))
                chain(dve.tensor_copy(c3[:, :, 0, :], c9[:, :, 0:E]))
                chain(dve.tensor_tensor(cres[:, :, :], c9[:, :, 0:E], c3[:, :, 0, :], ALU.subtract))
                chain(dve.tensor_copy(c3[:, :, 1, :], cres[:, :, :]))
                dve.tensor_tensor(c3[:, :, 2, :], cres[:, :, :], c3[:, :, 1, :], ALU.subtract).then_inc(c_ready, 1)
                for e in range(E):
                    dve.wait_ge(cb_full, 8 * u + e + 1)
                    dve.wait_ge(he_ready, 9 * u + e + 1)
                    if e >= 2:
                        dve.wait_ge(down_done, 9 * u + e - 1)
                    dve.tensor_tensor(GE[e % 2][:, :], HE[e % 2][:, :], cols(2 + e % 2), ALU.mult).then_inc(ge_ready, 1)
                dve.wait_ge(yacc_full, u + 1)
                dve.tensor_tensor(h2[:, :], cols(7), h1[:, :], ALU.add).then_inc(h2_ready, 1)

            stage_a(0, 0)
            stage_a(0, 1)
            dve.wait_ge(zeroed, 9)
            steps(dve, step, chain, last=UNITS - 2)

        @block.tensor
        def _(pe):
            def stage_a(m, h):
                u = 2 * m + h
                for j in range(3):
                    pe.wait_ge(x_in[h][j], 16 * (m + 1))
                    for half in range(2):
                        n = 2 * j + half
                        ring_wait("x", u, n)
                        turn(n, [xt[h][0:NT[j], j, 128 * k:128 * k + 128] for k in range(4 * half, 4 * half + 4)], NT[j])
                pe.wait_ge(xt_ready, 6 * (u + 1))
                wait(pe, ge_ready, 8 * (u - 2) if not (isinstance(m, int) and m == 0) else 0)
                for r in range(2):
                    for g in range(4):
                        kp = 4 * r + g
                        mm = pe.matmul(bank[2][32 * g:32 * g + 32, 0:TOK], wof[:, kp, :], XT[:, kp, :],
                                       start=(r == 0), stop=(r == 1), skip_group_check=True)
                mm.then_inc(off4_full, 1)
                pe.wait_ge(off4_ready, u + 1)
                wait(pe, ot_read, u)
                for j in range(3):
                    mm = pe.matmul(bank[3][0:NT[j], 32 * j:32 * j + 32], off4[:, T0[j]:T0[j] + NT[j]], cs["stk"][:, :],
                                   start=True, stop=True)
                mm.then_inc(ot_full, 1)

            def ring_wait(kind, u, k):
                if kind == "x":
                    if k >= 2:
                        pe.wait_ge(xt_ready, 6 * u + k - 1)
                    elif isinstance(u, int) and u < 2:
                        wait(pe, xt_ready, 6 * u + k - 1)
                    else:
                        pe.wait_ge(vt_ready, 6 * (u - 2) + 5 + k)
                else:
                    if k >= 2:
                        pe.wait_ge(vt_ready, 6 * u + k - 1)
                    elif isinstance(u, int) and u >= UNITS - 1:
                        wait(pe, vt_ready, 6 * u + k - 1)
                    else:
                        pe.wait_ge(xt_ready, 6 * (u + 2) + k - 1)

            def turn(n, srcs, nrow):
                for i, src in enumerate(srcs):
                    mm = pe.transpose(bank[n % 2][:, i * nrow:(i + 1) * nrow], src, ident[0:nrow, 0:nrow])
                mm.then_inc(tp_full, 1)

            def layer_norm(n, src, b):
                pe.matmul(cols(b), center[:, :], src, start=True, stop=True).then_inc(hc_full, 1)
                pe.wait_ge(sq_ready, n + 1)
                for t in range(RN):
                    mm = pe.matmul(bank[6][0:RT, COLS + t:COLS + t + 1], SQ[:, RT * t:RT * t + RT], mean1[:, :],
                                   start=True, stop=True)
                mm.then_inc(var_full, 1)
                pe.wait_ge(diag_ready, n + 1)
                pe.matmul(cols(6), ones[0:RT, :], diag[:, :, :].rearrange("p t r -> p (t r)"),
                          start=True, stop=True).then_inc(rstd_full, 1)
                pe.wait_ge(z_ready, n + 1)

            def step(m, h):
                u = 2 * m + h
                for j in range(3):
                    pe.wait_ge(val_ready, 3 * u + j + 1)
                    for half in range(2):
                        n = 2 * j + half
                        ring_wait("v", u, n)
                        turn(n, [VAL[0:NT[j], j, 128 * k:128 * k + 128] for k in range(4 * half, 4 * half + 4)], NT[j])
                pe.wait_ge(vt_ready, 6 * (u + 1))
                wait(pe, outs_ready, u)
                for kp in range(KP):
                    mm = pe.matmul(bank[4][:, 0:TOK], wdef[:, kp, :], VT[:, kp, :], start=(kp == 0), stop=(kp == KP - 1))
                mm.then_inc(tok_full, 1)
                if not (isinstance(m, int) and m + 1 >= UNITS // 2):
                    stage_a(m + 1, h)
                pe.wait_ge(h0_ready, u + 1)
                layer_norm(2 * u, h0[:, :, :].rearrange("p b s -> p (b s)"), 5)
                for qk in range(2):
                    for par in range(2):
                        for g in range(4):
                            mm = pe.matmul(bank[5][32 * g:32 * g + 32, qk * S:qk * S + S], w1pad[:, qk, par, :],
                                           Z[:, 2 * g + par, :], start=(par == 0), stop=(par == 1), skip_group_check=True)
                mm.then_inc(hqk_full, 1)
                pe.matmul(cols(7), scoreB[:, :], Zf, start=True, stop=True).then_inc(y_full, 1)
                for b in range(NB):
                    mm = pe.matmul(bank[2 + b // 4][0:S, 128 * (b % 4):128 * (b % 4) + 128], Z[:, b, :], cs["wvT"][:, :],
                                   start=True, stop=True)
                mm.then_inc(v_full, 1)
                pe.wait_ge(y_ready, u + 1)
                for b in range(NB):
                    mm = pe.matmul(bank[4][0:S, S * b:S * b + S], Y[:, b, :], Z[:, b, :], start=True, stop=True)
                mm.then_inc(s_full, 1)
                for g in range(4):
                    pe.wait_ge(th_ready, 2 * u + g // 2 + 1)
                    for s in range(2):
                        q0 = QG * g + QG // 2 * s
                        q1 = min(q0 + QG // 2, S)
                        mm = pe.matmul(bank[(5, 7)[s]][32 * g:32 * g + NB, 0:(q1 - q0) * S], w2blk[:, :],
                                       TH[:, q0:q1, :].rearrange("p q k -> p (q k)"), start=True, stop=True)
                mm.then_inc(est_full, 1)
                pe.wait_ge(p_ready, u + 1)
                pe.sem_inc(passed, 1)
                for b in range(NB):
                    mm = pe.transpose(bank[6][0:S, S * b:S * b + S], PR[:, b, :], ident[0:S, 0:S])
                mm.then_inc(pt_full, 1)
                pe.wait_ge(pt_ready, u + 1)
                pe.wait_ge(v_ready, 2 * (u + 1))
                for b in range(NB):
                    mm = pe.matmul(bank[5][:, S * b:S * b + S], V[:, b, :], PT[:, S * b:S * b + S], start=True, stop=True)
                mm.then_inc(av_full, 1)
                pe.wait_ge(h1_ready, u + 1)
                layer_norm(2 * u + 1, h1[:, :], 7)
                for t in range(RN):
                    mm = pe.matmul(bank[4][0:RT, E * t:E * t + E], Zf[:, RT * t:RT * t + RT], cs["gwT"][:, :], start=True, stop=True)
                mm.then_inc(gl_full, 1)

                def up(e):
                    if e >= 2:
                        pe.wait_ge(he_ready, 9 * u + e - 1)
                    pe.matmul(cols(5 + e % 2), w1e[:, e, :], Zf, start=True, stop=True).then_inc(up_full, 1)

                def weights_of(e):
                    if e >= 2:
                        pe.wait_ge(ge_ready, 8 * u + e - 1)
                    pe.matmul(cols(2 + e % 2), selb[:, e, :], cT3[:, :], start=True, stop=True).then_inc(cb_full, 1)

                def down(e):
                    if e < E:
                        pe.wait_ge(ge_ready, 8 * u + e + 1)
                    else:
                        pe.wait_ge(he_ready, 9 * u + e + 1)
                    pe.matmul(cols(7), w2e[:, e, :], GE[e % 2][:, :] if e < E else HE[e % 2][:, :],
                              start=(e == 0), stop=False).then_inc(down_done, 1)

                up(0)
                up(1)
                pe.wait_ge(c_ready, u + 1)
                for t in range(RN):
                    mm = pe.transpose(bank2b[0:24, RT * t:RT * t + RT], c3[:, t, :, :].rearrange("p a e -> p (a e)"),
                                      identb[0:RT, 0:RT])
                mm.then_inc(ct_full, 1)
                for t in range(RN):
                    mm = pe.transpose(bank[3][0:9, RT * t:RT * t + RT], c9[:, t, :], ident[0:RT, 0:RT])
                mm.then_inc(ct_full, 1)
                pe.wait_ge(ct_ready, 2 * (u + 1))
                weights_of(0)
                weights_of(1)
                for e in range(9):
                    down(e)
                    if e + 2 < 9:
                        up(e + 2)
                    if e + 2 < E:
                        weights_of(e + 2)
                pe.matmul(cols(7), b2pad[:, :], cT9[:, :], start=False, stop=True).then_inc(yacc_full, 1)
                pe.wait_ge(h2_ready, u + 1)
                for t in range(RN):
                    mm = pe.transpose(bank[4][0:RT, 128 * t:128 * t + 128], h2[:, RT * t:RT * t + RT], ident[:, :])
                mm.then_inc(out_full, 1)

            pe.wait_ge(const_in, NCONST)
            pe.wait_ge(psum_zeroed, 8)
            pe.wait_ge(zeroed, 9)
            stage_a(0, 0)
            stage_a(0, 1)
            pe.wait_ge(blk_in, 16 * (NB + 1))
            pe.wait_ge(dve_consts, 6)
            pe.matmul(bank[5][:, 0:128], cs["wq"][:, :], cs["wk"][:, :], start=True, stop=True).then_inc(setup_psum, 1)
            pe.matmul(bank[6][:, 0:H], cs["wq"][:, :], cs["w1qT"][:, :], start=True, stop=True).then_inc(setup_psum, 1)
            pe.matmul(bank[7][:, 0:H], cs["wk"][:, :], cs["w1kT"][:, :], start=True, stop=True).then_inc(setup_psum, 1)
            pe.wait_ge(setup_mats, 5)
            steps(pe, step, last=UNITS - 2)


def kernel(**inputs):
    import numpy as np
    import concourse.bacc as bacc
    from concourse.bass_utils import run_bass_kernel_spmd

    f = np.float32
    a = {n: np.asarray(v) for n, v in inputs.items()}
    p = np.arange(128)

    def taps(w):
        o = w.shape[0]
        return w.transpose(2, 1, 0).reshape(KP, 2, C, o).transpose(1, 2, 0, 3).reshape(128, KP * o)

    pos = np.arange(S, dtype=f)[:, None]
    div = np.exp(np.arange(0, D, 2, dtype=f) * f(-np.log(10000.0) / D))
    pe = np.zeros((S, D), f)
    pe[:, 0::2] = np.sin(pos * div)
    pe[:, 1::2] = np.cos(pos * div)
    base = np.stack([(W0[j] + p // NB)[:, None] * K + np.arange(K)[None, :] for j in range(3)], 1).astype(f)
    sel = np.zeros((24, E, 128), f)
    for r in range(24):
        sel[r, r % E] = 1
    dydx = np.r_[np.arange(0, 32, 2), np.arange(1, 32, 2)]
    boff = a["L0_tok_b_off"][dydx]
    W1 = a["L0_attn_W1"]
    host = {
        "ident": np.eye(128, dtype=f), "wof": taps(a["L0_tok_w_off"][dydx]), "stk": np.tile(np.eye(32, dtype=f), (4, 1)),
        "boff": np.broadcast_to(boff, (128, 32)), "base": base.reshape(128, 48),
        "rowbase": np.repeat((p % NB * L)[:, None], 3, 1).astype(f), "wdef": taps(a["L0_tok_w_def"]),
        "bdef": a["L0_tok_b_def"][:, None], "cls": a["L0_tok_cls_token"].reshape(128, 1), "peT": pe.T,
        "center": (np.eye(128) - 1.0 / D).astype(f), "wq": a["L0_attn_Wq"], "wk": a["L0_attn_Wk"], "wvT": a["L0_attn_Wv"].T,
        "w1qT": W1[:, :D].T, "w1kT": W1[:, D:].T, "b1h": np.tile(a["L0_attn_b1"], NB)[:, None],
        "gwT": a["L0_ffn_gate_w"].T, "tri": np.broadcast_to(np.tril(np.ones((E, E), f), -1).reshape(1, 64), (128, 64)),
        "w1e": np.concatenate([a["L0_ffn_w1"], a["L0_ffn_sw1"][None]]).transpose(1, 0, 2).reshape(128, 9 * 128),
        "w2e": np.concatenate([a["L0_ffn_w2"], a["L0_ffn_sw2"][None]]).transpose(1, 0, 2).reshape(128, 9 * 128),
        "fb1": np.concatenate([a["L0_ffn_b1"], a["L0_ffn_sb1"][None]]).T, "sel": sel.reshape(24, E * 128),
        "b2col": np.broadcast_to(a["L0_attn_b2"], (128, 1)),
        "w2col": a["L0_attn_W2"].T, "b2e": np.concatenate([a["L0_ffn_b2"], a["L0_ffn_sb2"][None]]),
        "x": a["x"].reshape(B, L * C),
    }
    nc = bacc.Bacc("TRN2", target_bir_lowering=False, num_devices=1)
    arrays, aps = {}, {}
    for name, v in host.items():
        v = np.ascontiguousarray(v)
        arrays[f"in_{name}"] = v
        aps[name] = nc.dram_tensor(f"in_{name}", v.shape, mybir.dt.from_np(v.dtype), kind="ExternalInput").ap()
    out = nc.dram_tensor("out_0", (B * S, D), mybir.dt.float32, kind="ExternalOutput").ap()
    audio_tower(nc, aps["x"], aps, aps, out)
    r = run_bass_kernel_spmd(nc, [arrays], core_ids=[0])
    return r.results[0]["out_0"].reshape(B, S, D)
```

```python
import concourse.bass as bass
from concourse import mybir
from contextlib import ExitStack

B, L, C = 128, 750, 64
K = 16
W = L // K
D = 128
S = W + 1
NB = 8
UNITS = B // NB
WT = [16, 16, 14]
W0 = [0, 16, 32]
NT = [NB * w for w in WT]
T0 = [0, 128, 256]
TOK = NB * W
COLS = NB * S
KP = K // 2
H = 16
E = 8
RT = 94
RN = COLS // RT
KH = 24
EPS = 1e-5
ROUND = 8388608.0

CONSTS = [
    ("ident", [128, 128]), ("wof", [128, KP * 32]), ("stk", [128, 32]), ("boff", [128, 32]),
    ("base", [128, 3 * K]), ("rowbase", [128, 3]),
    ("wdef", [128, KP * D]), ("bdef", [128, 1]), ("cls", [128, 1]),
    ("peT", [128, S]), ("center", [128, 128]), ("wq", [128, 128]), ("wk", [128, 128]), ("wvT", [128, 128]),
    ("w1qT", [128, H]), ("w1kT", [128, H]), ("b1h", [128, 1]), ("gwT", [128, E]), ("tri", [128, E * E]),
    ("w1e", [128, 9 * 128]), ("w2e", [128, 9 * 128]), ("fb1", [128, 9]), ("sel", [24, E * 128]), ("b2col", [128, 1]),
]
ROWS = [("w2col", [H, 1]), ("b2e", [9, 128])]

AHEAD = {"m": 0, "f": -1, "c": 1, "b": 1, "a": 3}
ORDER = {
    "tensor": ("fc m0 f0 m1 f1 f2 m2 f3 m3 b0 m4 f4 m5 f5 b1 f6 m7 f7 m8 b2 m9 m10 b3 m11 a0 m12 a1 f8 "
               "a2 f9 a3 f10 a4").split(),
    "scalar": ("fc m0 f0 f1 f2 f3 m3 m4 m5 b0 f4 m6 f5 f6 m7 b1 f7 b2 m9 a0 m12 a1 f8 a2 a3 f10").split(),
    "vector": ("f0 m1 f1 f2 m2 c0 m3 m4 f3 c1 m6 f4 m7 f5 c2 m8 m10 f6 f7 b3 m11 m12 m13 f9 m14 a4").split(),
    "sync": ("f10 a0").split(),
}
END_ORDER = {
    UNITS - 2: {
        "tensor": ("m0 m1 fc f0 m2 m3 f1 m4 f2 m5 f3 f4 m7 f5 m8 f6 m9 m10 b0 f7 f8 f9 b1 m11 b2 m12 f10 "
                   "b3").split(),
        "scalar": ("m0 fc f0 m3 f1 m4 m5 f2 f3 m6 f4 m7 f5 f6 m9 f7 f8 b0 b1 b2 m12 f10").split(),
        "vector": ("m1 m2 m3 m4 f0 f1 c0 f2 m6 m7 f3 f4 c1 m8 f5 f6 m10 f7 c2 m11 f9 m12 m13 m14 b3").split(),
        "sync": ("f10").split(),
    },
    UNITS - 1: {
        "tensor": ("fc m0 m1 f0 f1 m2 m3 m4 m5 f2 f3 m7 m8 m9 m10 f4 m11 m12 f5 f6 f7 f8 f9 f10").split(),
        "scalar": ("fc m0 f0 f1 m3 m4 m5 m6 f2 m7 f3 m9 f4 m12 f5 f6 f7 f8 f10").split(),
        "vector": ("m1 f0 f1 m2 m3 m4 m6 m7 f2 f3 m8 m10 m11 f4 m12 m13 f5 f6 f7 m14 f9").split(),
        "sync": ("f10").split(),
    },
}


def wait(eng, sem, n):
    if isinstance(n, int) and n <= 0:
        return
    eng.wait_ge(sem, n)


class Chain:

    def __init__(self, eng, sem):
        self.eng, self.sem, self.base, self.n = eng, sem, 0, 0

    def __call__(self, ins):
        ins.then_inc(self.sem, 1)
        self.n += 1
        self.eng.wait_ge(self.sem, self.base + self.n)

    def mark(self):
        self.at = self.n

    def loop(self, i, first, per):
        self.outer = self.base + self.n
        self.base, self.n = self.outer + (i - first) * per, 0

    def end(self, trips, per):
        assert self.n == per, (self.n, per)
        self.base, self.n = self.outer + trips * per, 0


def audio_tower(nc, x, consts, rows, out):
    fp32, bf16, i32 = mybir.dt.float32, mybir.dt.bfloat16, mybir.dt.int32
    ALU, ACT, AX = mybir.AluOpType, mybir.ActivationFunctionType, mybir.AxisListType

    ctx = ExitStack()
    with ctx:
        def sb(name, shape, dt=fp32):
            return ctx.enter_context(nc.sbuf_tensor(name, shape, dt))

        def sem(name):
            return ctx.enter_context(nc.semaphore(name))

        cs = {name: sb("c_" + name, shape) for name, shape in CONSTS}
        ident, center = cs["ident"], cs["center"]
        wof = cs["wof"][:, :].rearrange("p (k o) -> p k o", o=32)
        wdef = cs["wdef"][:, :].rearrange("p (k d) -> p k d", d=D)
        w1e = cs["w1e"][:, :].rearrange("p (e f) -> p e f", f=128)
        w2e = cs["w2e"][:, :].rearrange("p (e f) -> p e f", f=128)
        base = cs["base"][:, :].rearrange("p (j k) -> p j k", k=K)
        identb = sb("identb", [128, 128], bf16)
        selb = sb("selb", [24, E, 128], bf16)
        ones = sb("ones", [128, 128])
        mean1 = sb("mean1", [128, 1])
        scoreB = sb("scoreB", [128, 128])
        w1pad = sb("w1pad", [128, 2, 2, 32])
        w2blk = sb("w2blk", [128, NB])
        b2pad = sb("b2pad", [128, 128])
        pe_b = sb("pe_b", [128, S])
        cls_pe = sb("cls_pe", [128, 1])

        xt = [sb(f"xt{p}", [128, 3, K * C]) for p in range(2)]
        XT = sb("XT", [128, KP, TOK])
        off4 = sb("off4", [128, TOK])
        offs = sb("offs", [128, 3, 32])
        px = sb("px", [128, 3, K])
        nwy = sb("nwy", [128, 3, K])
        rr = sb("rr", [128, 3, K])
        e01 = sb("e01", [128, 3, K, 2])
        e01f = e01[:, :, :, :].rearrange("p j k s -> p (j k s)")
        rowb = sb("rowb", [128, 3])
        idx = [sb(f"idx{p}", [128, 3 * K], i32) for p in range(2)]
        aw = [sb(f"aw{p}", [128, 3, K, 2]) for p in range(2)]
        G = [sb(f"G{p}", [128, 3, K, 2 * C]) for p in range(2)]
        VAL = sb("VAL", [128, 3, K * C])
        VT = sb("VT", [128, KP, TOK])
        h0 = [sb(f"h0{p}", [128, NB, S]) for p in range(2)]
        SQ = sb("SQ", [128, COLS])
        HC = sb("HC", [128, COLS])
        Z = sb("Z", [128, NB, S])
        Zf = Z[:, :, :].rearrange("p b s -> p (b s)")
        Z2 = [sb(f"Z2{p}", [128, COLS]) for p in range(2)]
        var = sb("var", [RT, RN])
        nt_ = sb("nt_", [RT, RN])
        ry = sb("ry", [RT, RN])
        ishift = sb("ishift", [RT, RN], i32)
        diag = sb("diag", [RT, RN, RT])
        Y = sb("Y", [128, NB, S])
        V = sb("V", [128, NB, 128])
        hq = sb("hq", [128, S])
        hk = sb("hk", [128, S])
        TH = sb("TH", [128, S, S])
        SC = sb("SC", [S, NB, S])
        smx = sb("smx", [S, NB])
        ssum = sb("ssum", [S, NB])
        sinv = sb("sinv", [S, NB])
        PR = sb("PR", [S, NB, S])
        PT = sb("PT", [128, COLS])
        h1 = [sb(f"h1{p}", [128, COLS]) for p in range(2)]
        lg = sb("lg", [RT, RN, E])
        gmx = sb("gmx", [RT, RN])
        gp = sb("gp", [RT, RN, E])
        gsum = sb("gsum", [RT, RN])
        ginv = sb("ginv", [RT, RN])
        gt = sb("gt", [RT, RN, E, E])
        eq = sb("eq", [RT, RN, E, E])
        rank = sb("rank", [RT, RN, E])
        c9 = sb("c9", [RT, RN, 9])
        c3 = sb("c3", [RT, RN, 3, E], bf16)
        cres = sb("cres", [RT, RN, E])
        cT3 = sb("cT3", [24, COLS], bf16)
        cT9 = sb("cT9", [128, COLS])
        HE = [sb(f"HE{i}", [128, COLS]) for i in range(4)]
        CW = [sb(f"CW{i}", [128, COLS]) for i in range(3)]
        GE = [sb(f"GE{i}", [128, COLS]) for i in range(3)]
        h2 = sb("h2", [128, COLS])
        OUTS = [sb(f"OUTS{p}", [RT, RN, 128]) for p in range(2)]

        bank = [ctx.enter_context(nc.psum_tensor(f"bank{i}", [128, 512], fp32)) for i in range(8)]

        bank3b = bank[3][:, :].bitcast(bf16)

        def cols(t):
            return bank[t][:, 0:COLS]

        const_in, zeroed, psum_zeroed, setup_psum, setup_mats, dve_consts = (
            sem(n) for n in ("const_in", "zeroed", "psum_zeroed", "setup_psum", "setup_mats", "dve_consts"))
        blk_in = sem("blk_in")
        NFIRST = 6
        ident_in, first_in = sem("ident_in"), sem("first_in")
        x_in = [[sem(f"x_in{p}{j}") for j in range(3)] for p in range(2)]
        gathered = [[sem(f"gathered{p}{j}") for j in range(3)] for p in range(2)]
        out_done = [sem(f"out_done{p}") for p in range(2)]
        tp_full = sem("tp_full")
        xt_ready, vt_ready = sem("xt_ready"), sem("vt_ready")
        off4_full, off4_ready, ot_full, ot_read, idx_ready = (
            sem(n) for n in ("off4_full", "off4_ready", "ot_full", "ot_read", "idx_ready"))
        val_ready, tok_full, h0_ready = (sem(n) for n in ("val_ready", "tok_full", "h0_ready"))
        hc_full, sq_ready, hc_ready, var_full, diag_ready, rstd_full, z_ready = (
            sem(n) for n in ("hc_full", "sq_ready", "hc_ready", "var_full", "diag_ready", "rstd_full", "z_ready"))
        hqk_full, y_full, y_ready, v_full, v_ready, add_ready, th_ready = (
            sem(n) for n in ("hqk_full", "y_full", "y_ready", "v_full", "v_ready", "add_ready", "th_ready"))
        s_full, sc_ready, exp_ready, p_ready, pt_full, pt_ready, av_full, h1_ready = (
            sem(n) for n in ("s_full", "sc_ready", "exp_ready", "p_ready", "pt_full",
                             "pt_ready", "av_full", "h1_ready"))
        gl_full, lg_ready, gexp_ready, c_ready, ct_full, ct_ready = (
            sem(n) for n in ("gl_full", "lg_ready", "gexp_ready", "c_ready", "ct_full", "ct_ready"))
        up_full, he_ready, cb_full, ge_ready, down_done, yacc_full, h2_ready, out_full, outs_ready = (
            sem(n) for n in ("up_full", "he_ready", "cb_full", "ge_ready", "down_done", "yacc_full", "h2_ready",
                             "out_full", "outs_ready"))
        cw_ready = sem("cw_ready")
        passed = sem("passed")
        dve_chain, act_chain = sem("dve_chain"), sem("act_chain")

        def groups_x(m, h):
            return 6 * h if isinstance(m, int) and m == 0 else 12 * (2 * m + h) - 6

        def groups_v(u):
            if isinstance(u, int) and u == UNITS - 1:
                return 12 * u + 6
            return 12 * u + 12

        def steps(eng, engine, pieces, chain=None, last=(UNITS - 4) // 2):
            def step(i, t):
                for name in (END_ORDER.get(t, ORDER) if isinstance(i, int) else ORDER)[engine]:
                    v = t + AHEAD[name[0]]
                    if not isinstance(i, int):
                        pieces[name](i + v // 2, v % 2)
                    elif 0 <= v < UNITS:
                        pieces[name](v // 2, v % 2)

            for s in (-1, 0):
                step(0, s)
            if chain:
                chain.mark()
            for s in (1, 2):
                step(0, s)
            per = chain.n - chain.at if chain else 0
            with eng.Fori(1, last) as i:
                if chain:
                    chain.loop(i, 1, per)
                for r in (1, 2):
                    step(i, r)
            if chain:
                chain.end(last - 1, per)
            for s in range(2 * last + 1, UNITS + 1):
                step(0, s)

        block = ctx.enter_context(nc.Block())

        @block.sync
        def _(sp):
            def load_x(m, h):
                u = 2 * m + h
                for j in range(3):
                    if not (isinstance(m, int) and m == 0):
                        sp.wait_ge(tp_full, groups_x(m - 1, h) + 2 * (j + 1))
                    src = x[bass.ds(NB * u, NB), W0[j] * K * C:(W0[j] + WT[j]) * K * C]
                    sp.dma_start(xt[h][0:NT[j], j, :],
                                 src.rearrange("b (w n) -> w b n", w=WT[j])).then_inc(x_in[h][j], 16)

            def next_x(m, h):
                m, h = m + (h + 1) // 2, (h + 1) % 2
                if not (isinstance(m, int) and 2 * m + h >= UNITS):
                    load_x(m, h)

            def store(m, h):
                u = 2 * m + h
                sp.wait_ge(outs_ready, u + 1)
                sp.dma_start(out[bass.ds(COLS * u, COLS), :].rearrange("(t r) d -> r t d", r=RT),
                             OUTS[h][:, :, :]).then_inc(out_done[h], 16)

            load_x(0, 0)
            load_x(0, 1)
            for name, _s in CONSTS[NFIRST:]:
                sp.dma_start(cs[name][:, :], consts[name]).then_inc(const_in, 16)
            sp.wait_ge(zeroed, 2)
            for b in range(NB):
                sp.dma_start(w2blk[H * b:H * b + H, b:b + 1], rows["w2col"]).then_inc(blk_in, 16)
            sp.dma_start(b2pad[0:9, :], rows["b2e"]).then_inc(blk_in, 16)
            load_x(1, 0)
            steps(sp, "sync", {"a0": next_x, "f10": store}, last=(UNITS - 4) // 2 - 1)
            for h in range(2):
                sp.wait_ge(out_done[h], 16 * UNITS // 2)

        @block.gpsimd
        def _(pool):
            pool.memset(w2blk[:, :], 0.0).then_inc(zeroed, 1)
            pool.memset(b2pad[:, :], 0.0).then_inc(zeroed, 1)
            pool.memset(w1pad[:, :, :, :], 0.0).then_inc(zeroed, 1)
            pool.memset(PT[:, :], 0.0).then_inc(zeroed, 1)
            pool.memset(V[:, :, :], 0.0).then_inc(zeroed, 1)
            pool.memset(cT9[:, :], 0.0).then_inc(zeroed, 1)
            pool.memset(c9[:, :, :], 1.0).then_inc(zeroed, 1)
            pool.memset(ones[:, :], 1.0).then_inc(zeroed, 1)
            pool.memset(mean1[:, :], 1.0 / D).then_inc(zeroed, 1)

            def gathers(m, h):
                u = 2 * m + h
                pool.wait_ge(idx_ready, u + 1)
                for j in range(3):
                    if not (isinstance(m, int) and m == 0):
                        pool.wait_ge(val_ready, 3 * u - 5 + j)
                    pool.sem_inc(passed, 1)
                    for k in range(K):
                        col = j * K + k
                        pool.indirect_dma_start(
                            out=G[h][0:NT[j], j, k, :], out_offset=None, in_=x.rearrange("b (l c) -> (b l) c", c=C),
                            in_offset=bass.IndirectOffsetOnAxis(ap=idx[h][0:NT[j], col:col + 1], axis=0),
                        ).then_inc(gathered[h][j], 16)

            gathers(0, 0)
            gathers(0, 1)
            with pool.Fori(1, UNITS // 2) as i:
                gathers(i, 0)
                gathers(i, 1)

        @block.scalar
        def _(act):
            chain = Chain(act, act_chain)
            act.dma_start(ident[:, :], consts["ident"]).then_inc(ident_in, 16)
            for name, _s in CONSTS[1:NFIRST]:
                act.dma_start(cs[name][:, :], consts[name]).then_inc(first_in, 16)

            def evacuate(first, n, dst, nrow, ready):
                act.wait_ge(tp_full, first + n + 1)
                act.activation(dst, bank[n % 2][:, 0:4 * nrow].rearrange("p (k t) -> p k t", k=4), ACT.Copy).then_inc(ready, 1)

            def turned_x(j):
                def piece(m, h):
                    if j == 0:
                        wait(act, off4_full, 2 * m + h)
                    for half in range(2):
                        evacuate(groups_x(m, h), 2 * j + half, XT[:, 4 * half:4 * half + 4, T0[j]:T0[j] + NT[j]], NT[j], xt_ready)
                return piece

            def turned_values(j):
                def piece(m, h):
                    u = 2 * m + h
                    if j == 0:
                        wait(act, tok_full, u)
                    for half in range(2):
                        evacuate(groups_v(u), 2 * j + half, VT[:, 4 * half:4 * half + 4, T0[j]:T0[j] + NT[j]], NT[j], vt_ready)
                return piece

            def offsets_out(m, h):
                u = 2 * m + h
                wait(act, ot_full, u)
                act.wait_ge(off4_full, u + 1)
                act.activation(off4[:, :], bank[0][:, 0:TOK], ACT.Copy).then_inc(off4_ready, 1)

            def squares(second):
                def piece(m, h):
                    act.wait_ge(hc_full, 2 * (2 * m + h) + second + 1)
                    act.activation(SQ[:, :], cols(5), ACT.Square).then_inc(sq_ready, 1)
                    act.activation(HC[:, :], cols(5), ACT.Copy).then_inc(hc_ready, 1)
                return piece

            def value_rows(u, half):
                act.wait_ge(v_full, 2 * u + half + 1)
                act.activation(V[0:S, 4 * half:4 * half + 4, :],
                               bank[6][0:S, :].rearrange("p (b n) -> p b n", b=4), ACT.Copy).then_inc(v_ready, 1)

            def hidden_tanh(u, half):
                act.wait_ge(add_ready, 2 * u + half + 1)
                k0, k1 = (0, KH) if half == 0 else (KH, S)
                act.activation(TH[:, k0:k1, :], TH[:, k0:k1, :], ACT.Tanh).then_inc(th_ready, 1)

            def m3(m, h):
                u = 2 * m + h
                act.wait_ge(y_full, u + 1)
                act.activation(Y[:, :, :].rearrange("p b s -> p (b s)"), cols(7), ACT.Copy).then_inc(y_ready, 1)
                value_rows(u, 0)

            def m4(m, h):
                u = 2 * m + h
                hidden_tanh(u, 0)
                value_rows(u, 1)

            def m5(m, h):
                hidden_tanh(2 * m + h, 1)

            def m6(m, h):
                act.wait_ge(sc_ready, 2 * m + h + 1)
                act.activation(SC[:, :, :], SC[:, :, :], ACT.Exp).then_inc(exp_ready, 1)

            def m7(m, h):
                act.wait_ge(pt_full, 2 * m + h + 1)
                act.activation(PT[0:S, :], bank[5][0:S, 0:COLS], ACT.Copy).then_inc(pt_ready, 1)

            def m12(m, h):
                act.wait_ge(lg_ready, 2 * m + h + 1)
                act.activation(lg[:, :, :], lg[:, :, :], ACT.Exp).then_inc(gexp_ready, 1)

            def fc(m, h):
                u = 2 * m + h
                wait(act, cb_full, 8 * u)
                act.wait_ge(ct_full, 2 * u + 1)
                act.activation(cT3[:, :], bank3b[0:24, 0:COLS], ACT.Copy).then_inc(ct_ready, 1)
                act.wait_ge(ct_full, 2 * u + 2)
                act.activation(cT9[0:9, :], bank[2][0:9, 0:COLS], ACT.Copy).then_inc(ct_ready, 1)

            def hidden(e):
                def piece(m, h):
                    u = 2 * m + h
                    act.wait_ge(up_full, 9 * u + e + 1)
                    if e == 0:
                        wait(act, down_done, 9 * u)
                    if e >= 4:
                        act.wait_ge(ge_ready, 8 * u + e - 3)
                    act.activation(HE[e % 4][:, :], cols(2), ACT.Relu, bias=cs["fb1"][:, e:e + 1]).then_inc(he_ready, 1)
                    if e < E:
                        act.wait_ge(cb_full, 8 * u + e + 1)
                        if e >= 3:
                            act.wait_ge(ge_ready, 8 * u + e - 2)
                        act.activation(CW[e % 3][:, :], cols(3), ACT.Copy).then_inc(cw_ready, 1)
                return piece

            def f10(m, h):
                act.wait_ge(out_full, 2 * m + h + 1)
                if not (isinstance(m, int) and m == 0):
                    act.wait_ge(out_done[h], 16 * m)
                act.activation(OUTS[h][:, :, :], bank[2][0:RT, :].rearrange("p (t n) -> p t n", t=RN),
                               ACT.Copy).then_inc(outs_ready, 1)

            act.wait_ge(psum_zeroed, 8)
            for h in range(2):
                for j in range(3):
                    turned_x(j)(0, h)
                offsets_out(0, h)
            act.wait_ge(setup_psum, 3)
            act.activation(scoreB[:, :], bank[5][:, 0:128], ACT.Copy, scale=float(D) ** -0.5).then_inc(setup_mats, 1)
            act.wait_ge(zeroed, 9)
            for qk in range(2):
                for par in range(2):
                    act.activation(w1pad[:, qk, par, H * par:H * par + H], bank[6 + qk][:, 0:H], ACT.Copy).then_inc(setup_mats, 1)
            pieces = {"m0": squares(0), "m3": m3, "m4": m4, "m5": m5, "m6": m6, "m7": m7, "m9": squares(1), "m12": m12,
                      "fc": fc, "f10": f10, "a3": offsets_out}
            pieces.update({f"a{j}": turned_x(j) for j in range(3)})
            pieces.update({f"b{j}": turned_values(j) for j in range(3)})
            pieces.update({f"f{e}": hidden(e) for e in range(9)})
            steps(act, "scalar", pieces)

        @block.vector
        def _(dve):
            chain = Chain(dve, dve_chain)
            for b in range(8):
                dve.memset(bank[b][:, :], 0.0).then_inc(psum_zeroed, 1)
            dve.wait_ge(ident_in, 16)
            dve.wait_ge(first_in, 16 * (NFIRST - 1))
            dve.tensor_copy(identb[:, :], ident[:, :]).then_inc(dve_consts, 1)
            chain(dve.tensor_copy(rowb[:, :], cs["rowbase"][:, :]))
            dve.wait_ge(psum_zeroed, 8)

            def stage_a(m, h):
                u = 2 * m + h
                dve.wait_ge(ot_full, u + 1)
                dve.tensor_tensor(offs[:, :, :], bank[1][:, 0:96].rearrange("p (j o) -> p j o", o=32),
                                  cs["boff"][:, :].unsqueeze(1).broadcast_to([128, 3, 32]), ALU.add).then_inc(ot_read, 1)
                dve.wait_ge(ot_read, u + 1)
                chain(dve.tensor_tensor(px[:, :, :], offs[:, :, K:2 * K], base, ALU.add))
                chain(dve.scalar_tensor_tensor(nwy[:, :, :], offs[:, :, 0:K], -1.0, offs[:, :, 0:K], ALU.mult, ALU.max))
                chain(dve.tensor_scalar(rr[:, :, :], px[:, :, :], -0.5, 0.0, ALU.add, ALU.max))
                chain(dve.tensor_scalar(nwy[:, :, :], nwy[:, :, :], 1.0, 1.0, ALU.min, ALU.subtract))
                chain(dve.tensor_scalar(rr[:, :, :], rr[:, :, :], float(L - 2), ROUND, ALU.min, ALU.add))
                chain(dve.tensor_scalar(rr[:, :, :], rr[:, :, :], ROUND, None, ALU.subtract))
                chain(dve.tensor_tensor(idx[h][:, :].rearrange("p (j k) -> p j k", k=K), rr[:, :, :],
                                        rowb[:, :].unsqueeze(2).broadcast_to([128, 3, K]), ALU.add))
                chain(dve.tensor_tensor(e01[:, :, :, 0], px[:, :, :], rr[:, :, :], ALU.subtract))
                chain(dve.tensor_scalar(e01[:, :, :, 1], e01[:, :, :, 0], 1.0, None, ALU.subtract))
                chain(dve.scalar_tensor_tensor(e01f, e01f, -1.0, e01f, ALU.mult, ALU.max))
                chain(dve.tensor_scalar(e01f, e01f, 1.0, 1.0, ALU.min, ALU.subtract))
                chain(dve.tensor_scalar(rowb[:, :], rowb[:, :], float(NB * L), None, ALU.add))
                dve.tensor_tensor(aw[h][:, :, :, :], e01[:, :, :, :], nwy[:, :, :].unsqueeze(3).broadcast_to([128, 3, K, 2]),
                                  ALU.mult).then_inc(idx_ready, 1)

            def rstd(second):
                def piece(m, h):
                    dve.wait_ge(var_full, 2 * (2 * m + h) + second + 1)
                    chain(dve.tensor_scalar(var[:, :], bank[6][0:RT, COLS:COLS + RN], EPS, None, ALU.add))
                    chain(dve.tensor_scalar(ishift[:, :], var[:, :].bitcast(i32), 1, None, ALU.logical_shift_right))
                    chain(dve.tensor_scalar(ry[:, :].bitcast(i32), ishift[:, :], -1.0, float(0x5F3759DF), ALU.mult, ALU.add))
                    for _i in range(3):
                        chain(dve.scalar_tensor_tensor(nt_[:, :], ry[:, :], -0.5, ry[:, :], ALU.mult, ALU.mult))
                        chain(dve.tensor_tensor(nt_[:, :], nt_[:, :], var[:, :], ALU.mult))
                        chain(dve.scalar_tensor_tensor(ry[:, :], nt_[:, :], 1.5, ry[:, :], ALU.add, ALU.mult))
                    dve.tensor_tensor(diag[:, :, :], ident[0:RT, 0:RT].unsqueeze(1).broadcast_to([RT, RN, RT]),
                                      ry[:, :].unsqueeze(2).broadcast_to([RT, RN, RT]), ALU.mult).then_inc(diag_ready, 1)
                return piece

            def normalize(second):
                def piece(m, h):
                    n = 2 * (2 * m + h) + second
                    dve.wait_ge(rstd_full, n + 1)
                    dve.wait_ge(hc_ready, n + 1)
                    dve.tensor_tensor(Z2[h][:, :] if second else Zf, HC[:, :], cols(6), ALU.mult).then_inc(z_ready, 1)
                return piece

            def combine(j):
                def piece(m, h):
                    u = 2 * m + h
                    dve.wait_ge(gathered[h][j], 16 * K * (m + 1))
                    g = G[h][0:NT[j], j, :, :].rearrange("p k (s c) -> p (k s) c", s=2)
                    w = aw[h][0:NT[j], j, :, :].rearrange("p k s -> p (k s)").unsqueeze(2).broadcast_to([NT[j], 2 * K, C])
                    chain(dve.tensor_tensor(g, g, w, ALU.mult))
                    if not (isinstance(m, int) and u == 0):
                        dve.wait_ge(tp_full, groups_v(u - 1) + 2 * (j + 1))
                    g = G[h][0:NT[j], j, :, :]
                    dve.tensor_tensor(VAL[0:NT[j], j, :].rearrange("p (k c) -> p k c", c=C), g[:, :, 0:C],
                                      g[:, :, C:2 * C], ALU.add).then_inc(val_ready, 1)
                return piece

            def b3(m, h):
                dve.wait_ge(tok_full, 2 * m + h + 1)
                for j in range(3):
                    s0 = 1 + W0[j]
                    ins = dve.tensor_tensor(
                        h0[h][:, :, s0:s0 + WT[j]].rearrange("p b s -> p s b"),
                        bank[0][:, T0[j]:T0[j] + NT[j]].rearrange("p (w b) -> p w b", b=NB),
                        pe_b[:, s0:s0 + WT[j]].unsqueeze(2).broadcast_to([128, WT[j], NB]), ALU.add)
                ins.then_inc(h0_ready, 1)

            def m3(m, h):
                dve.wait_ge(hqk_full, 2 * m + h + 1)
                chain(dve.tensor_scalar(hq[:, :], bank[5][:, 0:S], cs["b1h"][:, 0:1], None, ALU.add))
                chain(dve.tensor_copy(hk[:, :], bank[5][:, S:2 * S]))
                pair_sums(0)

            def pair_sums(half):
                k0, k1 = (0, KH) if half == 0 else (KH, S)
                dve.tensor_tensor(TH[:, k0:k1, :], hq[:, :].unsqueeze(1).broadcast_to([128, k1 - k0, S]),
                                  hk[:, k0:k1].unsqueeze(2).broadcast_to([128, k1 - k0, S]), ALU.add).then_inc(add_ready, 1)

            def m4(m, h):
                pair_sums(1)

            def m6(m, h):
                dve.wait_ge(s_full, 2 * m + h + 1)
                sc = bank[6][0:S, 0:COLS].rearrange("p (b s) -> p b s", b=NB)
                chain(dve.reduce_max(smx[:, :], sc, AX.X))
                chain(dve.tensor_scalar(smx[:, :], smx[:, :], cs["b2col"][0:S, 0:1], None, ALU.add))
                dve.scalar_tensor_tensor(SC[:, :, :], sc, cs["b2col"][0:S, 0:1],
                                         smx[:, :].unsqueeze(2).broadcast_to([S, NB, S]), ALU.add,
                                         ALU.subtract).then_inc(sc_ready, 1)

            def m7(m, h):
                dve.wait_ge(exp_ready, 2 * m + h + 1)
                chain(dve.reduce_sum(ssum[:, :], SC[:, :, :], AX.X))
                chain(dve.reciprocal(sinv[:, :], ssum[:, :]))
                dve.tensor_tensor(PR[:, :, :], SC[:, :, :], sinv[:, :].unsqueeze(2).broadcast_to([S, NB, S]),
                                  ALU.mult).then_inc(p_ready, 1)

            def m8(m, h):
                dve.wait_ge(av_full, 2 * m + h + 1)
                dve.tensor_tensor(h1[h][:, :], cols(7), h0[h][:, :, :].rearrange("p b s -> p (b s)"), ALU.add).then_inc(h1_ready, 1)

            def m12(m, h):
                u = 2 * m + h
                dve.wait_ge(gl_full, u + 1)
                glv = bank[7][0:RT, 0:RN * E].rearrange("p (t e) -> p t e", e=E)
                chain(dve.reduce_max(gmx[:, :], glv, AX.X))
                dve.tensor_tensor(lg[:, :, :], glv, gmx[:, :].unsqueeze(2).broadcast_to([RT, RN, E]),
                                  ALU.subtract).then_inc(lg_ready, 1)

            def m13(m, h):
                dve.wait_ge(gexp_ready, 2 * m + h + 1)
                chain(dve.reduce_sum(gsum[:, :], lg[:, :, :], AX.X))
                chain(dve.reciprocal(ginv[:, :], gsum[:, :]))
                chain(dve.tensor_tensor(gp[:, :, :], lg[:, :, :], ginv[:, :].unsqueeze(2).broadcast_to([RT, RN, E]), ALU.mult))
                other = gp[:, :, :].unsqueeze(2).broadcast_to([RT, RN, E, E])
                own = gp[:, :, :].unsqueeze(3).broadcast_to([RT, RN, E, E])
                chain(dve.tensor_tensor(eq[:, :, :, :], other, own, ALU.is_equal))
                chain(dve.tensor_tensor(eq[:, :, :, :].rearrange("p t i j -> p t (i j)"),
                                        eq[:, :, :, :].rearrange("p t i j -> p t (i j)"),
                                        cs["tri"][0:RT, :].unsqueeze(1).broadcast_to([RT, RN, E * E]), ALU.mult))
                chain(dve.tensor_tensor(gt[:, :, :, :], other, own, ALU.is_gt))
                chain(dve.tensor_tensor(gt[:, :, :, :], gt[:, :, :, :], eq[:, :, :, :], ALU.add))
                chain(dve.reduce_sum(rank[:, :, :], gt[:, :, :, :], AX.X))

            def m14(m, h):
                chain(dve.scalar_tensor_tensor(gp[:, :, :], rank[:, :, :], 2.0, gp[:, :, :], ALU.is_lt, ALU.mult))
                chain(dve.reduce_sum(gsum[:, :], gp[:, :, :], AX.X))
                chain(dve.tensor_scalar(gsum[:, :], gsum[:, :], 1e-20, None, ALU.add))
                chain(dve.reciprocal(ginv[:, :], gsum[:, :]))
                chain(dve.tensor_tensor(c9[:, :, 0:E], gp[:, :, :], ginv[:, :].unsqueeze(2).broadcast_to([RT, RN, E]), ALU.mult))
                chain(dve.tensor_copy(c3[:, :, 0, :], c9[:, :, 0:E]))
                chain(dve.tensor_tensor(cres[:, :, :], c9[:, :, 0:E], c3[:, :, 0, :], ALU.subtract))
                chain(dve.tensor_copy(c3[:, :, 1, :], cres[:, :, :]))
                dve.tensor_tensor(c3[:, :, 2, :], cres[:, :, :], c3[:, :, 1, :], ALU.subtract).then_inc(c_ready, 1)

            def weighted(e):
                def piece(m, h):
                    u = 2 * m + h
                    dve.wait_ge(cw_ready, 8 * u + e + 1)
                    dve.wait_ge(he_ready, 9 * u + e + 1)
                    if e >= 3:
                        dve.wait_ge(down_done, 9 * u + e - 2)
                    dve.tensor_tensor(GE[e % 3][:, :], HE[e % 4][:, :], CW[e % 3][:, :], ALU.mult).then_inc(ge_ready, 1)
                return piece

            def f9(m, h):
                dve.wait_ge(yacc_full, 2 * m + h + 1)
                dve.tensor_tensor(h2[:, :], cols(4), h1[h][:, :], ALU.add).then_inc(h2_ready, 1)

            stage_a(0, 0)
            stage_a(0, 1)
            dve.wait_ge(const_in, 16 * (len(CONSTS) - NFIRST))
            dve.tensor_copy(selb[:, :, :].rearrange("p e n -> p (e n)"), cs["sel"][:, :]).then_inc(dve_consts, 1)
            dve.tensor_scalar(pe_b[:, :], cs["peT"][:, :], cs["bdef"][:, 0:1], None, ALU.add).then_inc(dve_consts, 1)
            dve.tensor_tensor(cls_pe[:, :], cs["cls"][:, :], cs["peT"][:, 0:1], ALU.add).then_inc(dve_consts, 1)
            dve.wait_ge(dve_consts, 4)
            for p in range(2):
                chain(dve.tensor_copy(h0[p][:, :, 0:1], cls_pe[:, :].unsqueeze(1).broadcast_to([128, NB, 1])))
            dve.wait_ge(zeroed, 9)
            pieces = {"m1": rstd(0), "m2": normalize(0), "m3": m3, "m4": m4, "m6": m6, "m7": m7, "m8": m8, "m10": rstd(1),
                      "m11": normalize(1), "m12": m12, "m13": m13, "m14": m14, "f9": f9, "b3": b3, "a4": stage_a}
            pieces.update({f"c{j}": combine(j) for j in range(3)})
            pieces.update({f"f{e}": weighted(e) for e in range(E)})
            steps(dve, "vector", pieces, chain)

        @block.tensor
        def _(pe):
            def turn(n, srcs, nrow):
                for i, src in enumerate(srcs):
                    mm = pe.transpose(bank[n % 2][:, i * nrow:(i + 1) * nrow], src, ident[0:nrow, 0:nrow])
                mm.then_inc(tp_full, 1)

            def four(t, j, half):
                return [t[0:NT[j], j, 128 * k:128 * k + 128] for k in range(4 * half, 4 * half + 4)]

            def turn_x(j):
                def piece(m, h):
                    u = 2 * m + h
                    pe.wait_ge(x_in[h][j], 16 * (m + 1))
                    for n in (2 * j, 2 * j + 1):
                        if n >= 2:
                            pe.wait_ge(xt_ready, 6 * u + n - 1)
                        elif n == 0 and not (isinstance(m, int) and m == 0):
                            pe.wait_ge(h0_ready, u - 1)
                        elif n == 1 and isinstance(m, int) and u == 1:
                            pe.wait_ge(ot_read, 1)
                        turn(n, four(xt[h], j, n % 2), NT[j])
                return piece

            def turn_values(j):
                def piece(m, h):
                    u = 2 * m + h
                    last = isinstance(m, int) and u == UNITS - 1
                    pe.wait_ge(val_ready, 3 * u + j + 1)
                    for n in (2 * j, 2 * j + 1):
                        if n >= 2:
                            pe.wait_ge(vt_ready, 6 * u + n - 1)
                        elif n == 0 and last:
                            pe.wait_ge(h0_ready, u)
                        elif n == 1 and not last:
                            pe.wait_ge(ot_read, u + 2)
                        turn(n, four(VAL, j, n % 2), NT[j])
                return piece

            def b3(m, h):
                pe.wait_ge(vt_ready, 6 * (2 * m + h + 1))
                for kp in range(KP):
                    mm = pe.matmul(bank[0][:, 0:TOK], wdef[:, kp, :], VT[:, kp, :], start=(kp == 0), stop=(kp == KP - 1))
                mm.then_inc(tok_full, 1)

            def a3(m, h):
                pe.wait_ge(xt_ready, 6 * (2 * m + h + 1))
                for r in range(2):
                    for g in range(4):
                        kp = 4 * r + g
                        mm = pe.matmul(bank[0][32 * g:32 * g + 32, 0:TOK], wof[:, kp, :], XT[:, kp, :],
                                       start=(r == 0), stop=(r == 1), skip_group_check=True)
                mm.then_inc(off4_full, 1)

            def a4(m, h):
                pe.wait_ge(off4_ready, 2 * m + h + 1)
                for j in range(3):
                    mm = pe.matmul(bank[1][0:NT[j], 32 * j:32 * j + 32], off4[:, T0[j]:T0[j] + NT[j]], cs["stk"][:, :],
                                   start=True, stop=True)
                mm.then_inc(ot_full, 1)

            def centered(second):
                def piece(m, h):
                    if second:
                        pe.wait_ge(h1_ready, 2 * m + h + 1)
                        src = h1[h][:, :]
                    else:
                        pe.wait_ge(h0_ready, 2 * m + h + 1)
                        src = h0[h][:, :, :].rearrange("p b s -> p (b s)")
                    pe.matmul(cols(5), center[:, :], src, start=True, stop=True).then_inc(hc_full, 1)
                return piece

            def variance(second):
                def piece(m, h):
                    pe.wait_ge(sq_ready, 2 * (2 * m + h) + second + 1)
                    for t in range(RN):
                        mm = pe.matmul(bank[6][0:RT, COLS + t:COLS + t + 1], SQ[:, RT * t:RT * t + RT], mean1[:, :],
                                       start=True, stop=True)
                    mm.then_inc(var_full, 1)
                return piece

            def spread_rstd(second):
                def piece(m, h):
                    pe.wait_ge(diag_ready, 2 * (2 * m + h) + second + 1)
                    pe.matmul(cols(6), ones[0:RT, :], diag[:, :, :].rearrange("p t r -> p (t r)"),
                              start=True, stop=True).then_inc(rstd_full, 1)
                return piece

            def values(u, half):
                for b in range(4 * half, 4 * half + 4):
                    mm = pe.matmul(bank[6][0:S, 128 * (b % 4):128 * (b % 4) + 128], Z[:, b, :], cs["wvT"][:, :],
                                   start=True, stop=True)
                mm.then_inc(v_full, 1)

            def m3(m, h):
                u = 2 * m + h
                pe.wait_ge(z_ready, 2 * u + 1)
                for qk in range(2):
                    for par in range(2):
                        for g in range(4):
                            mm = pe.matmul(bank[5][32 * g:32 * g + 32, qk * S:qk * S + S], w1pad[:, qk, par, :],
                                           Z[:, 2 * g + par, :], start=(par == 0), stop=(par == 1), skip_group_check=True)
                mm.then_inc(hqk_full, 1)
                pe.matmul(cols(7), scoreB[:, :], Zf, start=True, stop=True).then_inc(y_full, 1)
                values(u, 0)

            def m4(m, h):
                u = 2 * m + h
                pe.wait_ge(v_ready, 2 * u + 1)
                values(u, 1)

            def m5(m, h):
                u = 2 * m + h
                pe.wait_ge(y_ready, u + 1)
                pe.wait_ge(v_ready, 2 * u + 2)
                for b in range(NB):
                    mm = pe.matmul(bank[6][0:S, S * b:S * b + S], Y[:, b, :], Z[:, b, :], start=(b == 0), stop=True,
                              skip_group_check=True)
                for k in range(S):
                    if k in (0, KH):
                        pe.wait_ge(th_ready, 2 * u + (1 if k == 0 else 2))
                    mm = pe.matmul(bank[6][0:S, k:k + S * (NB - 1) + 1:S], TH[:, k, :], w2blk[:, :],
                                   start=False, stop=True, skip_group_check=True)
                mm.then_inc(s_full, 1)

            def m7(m, h):
                pe.wait_ge(p_ready, 2 * m + h + 1)
                pe.sem_inc(passed, 1)
                for b in range(NB):
                    mm = pe.transpose(bank[5][0:S, S * b:S * b + S], PR[:, b, :], ident[0:S, 0:S])
                mm.then_inc(pt_full, 1)

            def m8(m, h):
                pe.wait_ge(pt_ready, 2 * m + h + 1)
                for b in range(NB):
                    mm = pe.matmul(bank[7][:, S * b:S * b + S], V[:, b, :], PT[:, S * b:S * b + S], start=True, stop=True)
                mm.then_inc(av_full, 1)

            def m12(m, h):
                u = 2 * m + h
                pe.wait_ge(z_ready, 2 * u + 2)
                for t in range(RN):
                    mm = pe.matmul(bank[7][0:RT, E * t:E * t + E], Z2[h][:, RT * t:RT * t + RT], cs["gwT"][:, :],
                                   start=True, stop=True)
                mm.then_inc(gl_full, 1)

            def fc(m, h):
                u = 2 * m + h
                pe.wait_ge(c_ready, u + 1)
                wait(pe, cw_ready, 8 * u)
                for t in range(RN):
                    mm = pe.transpose(bank3b[0:24, RT * t:RT * t + RT], c3[:, t, :, :].rearrange("p a e -> p (a e)"),
                                      identb[0:RT, 0:RT])
                mm.then_inc(ct_full, 1)
                wait(pe, outs_ready, u)
                for t in range(RN):
                    mm = pe.transpose(bank[2][0:9, RT * t:RT * t + RT], c9[:, t, :], ident[0:RT, 0:RT])
                mm.then_inc(ct_full, 1)

            def down(u, e):
                if e < E:
                    pe.wait_ge(ge_ready, 8 * u + e + 1)
                else:
                    pe.wait_ge(he_ready, 9 * u + e + 1)
                if e == 0:
                    wait(pe, h2_ready, u)
                pe.matmul(cols(4), w2e[:, e, :], GE[e % 3][:, :] if e < E else HE[e % 4][:, :],
                          start=(e == 0), stop=False).then_inc(down_done, 1)

            def expert(e):
                def piece(m, h):
                    u = 2 * m + h
                    if e == 0:
                        pe.wait_ge(ct_ready, 2 * (u + 1))
                    else:
                        pe.wait_ge(he_ready, 9 * u + e)
                    pe.matmul(cols(2), w1e[:, e, :], Z2[h][:, :], start=True, stop=True).then_inc(up_full, 1)
                    if e >= 2:
                        down(u, e - 2)
                    if e < E:
                        if e >= 1:
                            pe.wait_ge(cw_ready, 8 * u + e)
                        pe.matmul(cols(3), selb[:, e, :], cT3[:, :], start=True, stop=True).then_inc(cb_full, 1)
                return piece

            def f9(m, h):
                u = 2 * m + h
                down(u, 7)
                down(u, 8)
                pe.matmul(cols(4), b2pad[:, :], cT9[:, :], start=False, stop=True).then_inc(yacc_full, 1)

            def f10(m, h):
                pe.wait_ge(h2_ready, 2 * m + h + 1)
                for t in range(RN):
                    mm = pe.transpose(bank[2][0:RT, 128 * t:128 * t + 128], h2[:, RT * t:RT * t + RT], ident[:, :])
                mm.then_inc(out_full, 1)

            pe.wait_ge(ident_in, 16)
            pe.wait_ge(psum_zeroed, 8)
            for h in range(2):
                for j in range(3):
                    turn_x(j)(0, h)
                pe.wait_ge(first_in, 16 * (NFIRST - 1))
                a3(0, h)
                a4(0, h)
            pe.wait_ge(blk_in, 16 * (NB + 1))
            pe.wait_ge(const_in, 16 * (len(CONSTS) - NFIRST))
            pe.wait_ge(zeroed, 9)
            pe.wait_ge(dve_consts, 4)
            pe.matmul(bank[5][:, 0:128], cs["wq"][:, :], cs["wk"][:, :], start=True, stop=True).then_inc(setup_psum, 1)
            pe.matmul(bank[6][:, 0:H], cs["wq"][:, :], cs["w1qT"][:, :], start=True, stop=True).then_inc(setup_psum, 1)
            pe.matmul(bank[7][:, 0:H], cs["wk"][:, :], cs["w1kT"][:, :], start=True, stop=True).then_inc(setup_psum, 1)
            pe.wait_ge(setup_mats, 5)
            pieces = {"m0": centered(0), "m1": variance(0), "m2": spread_rstd(0), "m3": m3, "m4": m4, "m5": m5, "m7": m7,
                      "m8": m8, "m9": centered(1), "m10": variance(1), "m11": spread_rstd(1), "m12": m12,
                      "fc": fc, "f9": f9, "f10": f10, "b3": b3, "a3": a3, "a4": a4}
            pieces.update({f"a{j}": turn_x(j) for j in range(3)})
            pieces.update({f"b{j}": turn_values(j) for j in range(3)})
            pieces.update({f"f{e}": expert(e) for e in range(9)})
            steps(pe, "tensor", pieces)


def kernel(**inputs):
    import numpy as np
    import concourse.bacc as bacc
    from concourse.bass_utils import run_bass_kernel_spmd

    f = np.float32
    a = {n: np.asarray(v) for n, v in inputs.items()}
    p = np.arange(128)

    def taps(w):
        o = w.shape[0]
        return w.transpose(2, 1, 0).reshape(KP, 2, C, o).transpose(1, 2, 0, 3).reshape(128, KP * o)

    pos = np.arange(S, dtype=f)[:, None]
    div = np.exp(np.arange(0, D, 2, dtype=f) * f(-np.log(10000.0) / D))
    pe = np.zeros((S, D), f)
    pe[:, 0::2] = np.sin(pos * div)
    pe[:, 1::2] = np.cos(pos * div)
    base = np.stack([(W0[j] + p // NB)[:, None] * K + np.arange(K)[None, :] for j in range(3)], 1).astype(f)
    sel = np.zeros((24, E, 128), f)
    for r in range(24):
        sel[r, r % E] = 1
    dydx = np.r_[np.arange(0, 32, 2), np.arange(1, 32, 2)]
    boff = a["L0_tok_b_off"][dydx]
    W1 = a["L0_attn_W1"]
    host = {
        "ident": np.eye(128, dtype=f), "wof": taps(a["L0_tok_w_off"][dydx]), "stk": np.tile(np.eye(32, dtype=f), (4, 1)),
        "boff": np.broadcast_to(boff, (128, 32)), "base": base.reshape(128, 48),
        "rowbase": np.repeat((p % NB * L)[:, None], 3, 1).astype(f), "wdef": taps(a["L0_tok_w_def"]),
        "bdef": a["L0_tok_b_def"][:, None], "cls": a["L0_tok_cls_token"].reshape(128, 1), "peT": pe.T,
        "center": (np.eye(128) - 1.0 / D).astype(f), "wq": a["L0_attn_Wq"], "wk": a["L0_attn_Wk"], "wvT": a["L0_attn_Wv"].T,
        "w1qT": W1[:, :D].T, "w1kT": W1[:, D:].T, "b1h": np.tile(a["L0_attn_b1"], NB)[:, None],
        "gwT": a["L0_ffn_gate_w"].T, "tri": np.broadcast_to(np.tril(np.ones((E, E), f), -1).reshape(1, 64), (128, 64)),
        "w1e": np.concatenate([a["L0_ffn_w1"], a["L0_ffn_sw1"][None]]).transpose(1, 0, 2).reshape(128, 9 * 128),
        "w2e": np.concatenate([a["L0_ffn_w2"], a["L0_ffn_sw2"][None]]).transpose(1, 0, 2).reshape(128, 9 * 128),
        "fb1": np.concatenate([a["L0_ffn_b1"], a["L0_ffn_sb1"][None]]).T, "sel": sel.reshape(24, E * 128),
        "b2col": np.broadcast_to(a["L0_attn_b2"], (128, 1)),
        "w2col": a["L0_attn_W2"].T, "b2e": np.concatenate([a["L0_ffn_b2"], a["L0_ffn_sb2"][None]]),
        "x": a["x"].reshape(B, L * C),
    }
    nc = bacc.Bacc("TRN2", target_bir_lowering=False, num_devices=1)
    arrays, aps = {}, {}
    for name, v in host.items():
        v = np.ascontiguousarray(v)
        arrays[f"in_{name}"] = v
        aps[name] = nc.dram_tensor(f"in_{name}", v.shape, mybir.dt.from_np(v.dtype), kind="ExternalInput").ap()
    out = nc.dram_tensor("out_0", (B * S, D), mybir.dt.float32, kind="ExternalOutput").ap()
    audio_tower(nc, aps["x"], aps, aps, out)
    r = run_bass_kernel_spmd(nc, [arrays], core_ids=[0])
    return r.results[0]["out_0"].reshape(B, S, D)
```

```python
import concourse.bass as bass
from concourse import mybir
from contextlib import ExitStack

B, L, C = 128, 750, 64
K = 16
W = L // K
D = 128
S = W + 1
NB = 8
UNITS = B // NB
WT = [16, 16, 14]
W0 = [0, 16, 32]
NT = [NB * w for w in WT]
T0 = [0, 128, 256]
TOK = NB * W
COLS = NB * S
KP = K // 2
H = 16
E = 8
RT = 94
RN = COLS // RT
KH = 24
EPS = 1e-5
ROUND = 8388608.0

CONSTS = [
    ("ident", [128, 128]), ("wof", [128, KP * 32]), ("stk", [128, 32]), ("boff", [128, 32]),
    ("base", [128, 3 * K]), ("rowbase", [128, 3]),
    ("wdef", [128, KP * D]), ("bdef", [128, 1]), ("cls", [128, 1]),
    ("peT", [128, S]), ("center", [128, 128]), ("wq", [128, 128]), ("wk", [128, 128]), ("wvT", [128, 128]),
    ("w1qT", [128, H]), ("w1kT", [128, H]), ("b1h", [128, 1]), ("gwT", [128, E]), ("tri", [128, E * E]),
    ("w1e", [128, 9 * 128]), ("w2e", [128, 9 * 128]), ("fb1", [128, 9]), ("sel", [24, E * 128]), ("b2col", [128, 1]),
]
NFIRST = 6

AHEAD = {"m": 0, "f": -1, "g": -1, "d": -1, "c": 1, "b": 1, "a": 3}
ORDER = {
    "tensor": ("fs gc m0 f0 m1 g0 ds f1 g1 g2 f2 g3 m2 g4 f3 m3 d0 m4 d1 m5 f4 g5 b0 g6 f5 d2 d3 m7 g7 "
               "f6 m8 f7 d4 m9 b1 m10 b2 d5 b3 m11 d6 a0 m12 a1 d7 a2 d8 a3 d9 a4").split(),
    "scalar": ("fs gc m0 f0 g0 f1 g1 g2 f2 g3 g4 m3 m4 m5 f3 g5 f4 m6 f5 g6 b0 g7 m7 f6 f7 m9 b1 b2 a0 "
               "m12 a1 a2 a3 d9").split(),
    "vector": ("m1 g0 g1 m2 m3 m4 c0 g2 m6 g3 g4 m7 c1 m8 c2 g5 g6 g7 m10 b3 m11 m12 m13 d8 m14 a4").split(),
    "sync": ("d9 a0").split(),
}
END_ORDER = {
    UNITS - 2: {
        "tensor": ("m0 fs m1 gc g0 g1 f0 g2 m2 f1 m3 f2 m4 g3 m5 g4 f3 g5 ds f4 d0 d1 d2 m7 f5 g6 m8 f6 "
                   "g7 m9 f7 m10 d3 d4 d5 d6 b0 m11 d7 b1 d8 b2 m12 b3 d9").split(),
        "scalar": ("m0 fs gc g0 g1 f0 f1 g2 m3 m4 m5 f2 g3 g4 f3 m6 f4 g5 m7 g6 f5 f6 m9 f7 g7 b0 b1 b2 "
                   "m12 d9").split(),
        "vector": ("m1 m2 m3 m4 c0 g0 g1 m6 g2 m7 c1 m8 g3 g4 g5 g6 m10 g7 c2 d8 m11 m12 m13 m14 b3").split(),
        "sync": ("d9").split(),
    },
    UNITS - 1: {
        "tensor": ("m0 fs m1 gc g0 f0 g1 ds f1 m2 f2 m3 g2 d0 m4 g3 f3 m5 g4 d1 g5 f4 d2 g6 f5 g7 m7 d3 "
                   "m8 f6 m9 f7 m10 d4 d5 d6 d7 d8 m11 d9 m12").split(),
        "scalar": ("m0 fs gc g0 f0 f1 g1 f2 m3 g2 m4 f3 m5 g3 g4 g5 m6 f4 g6 g7 m7 f5 f6 m9 f7 d9 m12").split(),
        "vector": ("m1 g0 m2 g1 m3 m4 g2 g3 m6 m7 m8 g4 g5 g6 g7 m10 d8 m11 m12 m13 m14").split(),
        "sync": ("d9").split(),
    },
    UNITS: {
        "tensor": ("fs f0 f1 f2 gc f3 g0 ds f4 g1 d0 g2 f5 g3 d1 g4 d2 g5 f6 g6 d3 f7 g7 d4 d5 d6 d7 d8 "
                   "d9").split(),
        "scalar": ("fs f0 f1 f2 gc f3 g0 g1 f4 g2 g3 f5 g4 g5 f6 g6 g7 f7 d9").split(),
        "vector": ("g0 g1 g2 g3 g4 g5 g6 g7 d8").split(),
        "sync": ("d9").split(),
    },
}


def wait(eng, sem, n):
    if isinstance(n, int) and n <= 0:
        return
    eng.wait_ge(sem, n)


class Chain:

    def __init__(self, eng, sem):
        self.eng, self.sem, self.base, self.n = eng, sem, 0, 0

    def __call__(self, ins):
        ins.then_inc(self.sem, 1)
        self.n += 1
        self.eng.wait_ge(self.sem, self.base + self.n)

    def mark(self):
        self.at = self.n

    def loop(self, i, first, per):
        self.outer = self.base + self.n
        self.base, self.n = self.outer + (i - first) * per, 0

    def end(self, trips, per):
        assert self.n == per, (self.n, per)
        self.base, self.n = self.outer + trips * per, 0


def audio_tower(nc, x, consts, rows, out):
    fp32, bf16, i32 = mybir.dt.float32, mybir.dt.bfloat16, mybir.dt.int32
    ALU, ACT, AX = mybir.AluOpType, mybir.ActivationFunctionType, mybir.AxisListType

    ctx = ExitStack()
    with ctx:
        def sb(name, shape, dt=fp32):
            return ctx.enter_context(nc.sbuf_tensor(name, shape, dt))

        def sem(name):
            return ctx.enter_context(nc.semaphore(name))

        cs = {name: sb("c_" + name, shape) for name, shape in CONSTS}
        ident, center = cs["ident"], cs["center"]
        wof = cs["wof"][:, :].rearrange("p (k o) -> p k o", o=32)
        wdef = cs["wdef"][:, :].rearrange("p (k d) -> p k d", d=D)
        w1e = cs["w1e"][:, :].rearrange("p (e f) -> p e f", f=128)
        w2e = cs["w2e"][:, :].rearrange("p (e f) -> p e f", f=128)
        base = cs["base"][:, :].rearrange("p (j k) -> p j k", k=K)
        identb = sb("identb", [128, 128], bf16)
        selb = sb("selb", [24, E, 128], bf16)
        ones = sb("ones", [128, 128])
        mean1 = sb("mean1", [128, 1])
        tables = sb("tables", [128, 1])
        scoreB = sb("scoreB", [128, 128])
        w1pad = sb("w1pad", [128, 2, 2, 32])
        w2blk = sb("w2blk", [128, NB])
        b2pad = sb("b2pad", [128, 128])
        pe_b = sb("pe_b", [128, S])
        cls_pe = sb("cls_pe", [128, 1])

        xt = [sb(f"xt{p}", [128, 3, K * C]) for p in range(2)]
        XT = sb("XT", [128, KP, TOK])
        off4 = sb("off4", [128, TOK])
        offs = sb("offs", [128, 3, 32])
        px = sb("px", [128, 3, K])
        nwy = sb("nwy", [128, 3, K])
        rr = sb("rr", [128, 3, K])
        e01 = sb("e01", [128, 3, K, 2])
        e01f = e01[:, :, :, :].rearrange("p j k s -> p (j k s)")
        rowb = sb("rowb", [128, 3])
        idx = [sb(f"idx{p}", [128, 3 * K], i32) for p in range(2)]
        aw = [sb(f"aw{p}", [128, 3, K, 2]) for p in range(2)]
        G = [sb(f"G{p}", [128, 3, K, 2 * C]) for p in range(2)]
        VAL = sb("VAL", [128, 3, K * C])
        VT = sb("VT", [128, KP, TOK])
        h0 = [sb(f"h0{p}", [128, NB, S]) for p in range(2)]
        SQ = sb("SQ", [128, COLS])
        HC = sb("HC", [128, COLS])
        Z = sb("Z", [128, NB, S])
        Zf = Z[:, :, :].rearrange("p b s -> p (b s)")
        Z2 = [sb(f"Z2{p}", [128, COLS]) for p in range(2)]
        var = sb("var", [RT, RN])
        nt_ = sb("nt_", [RT, RN])
        ry = sb("ry", [RT, RN])
        ishift = sb("ishift", [RT, RN], i32)
        diag = sb("diag", [RT, RN, RT])
        Y = sb("Y", [128, NB, S])
        V = sb("V", [128, NB, 128])
        hq = sb("hq", [128, S])
        hk = sb("hk", [128, S])
        TH = sb("TH", [128, S, S])
        SC = sb("SC", [S, NB, S])
        smx = sb("smx", [S, NB])
        ssum = sb("ssum", [S, NB])
        sinv = sb("sinv", [S, NB])
        PR = sb("PR", [S, NB, S])
        PT = sb("PT", [128, COLS])
        h1 = [sb(f"h1{p}", [128, COLS]) for p in range(2)]
        lg = sb("lg", [RT, RN, E])
        eg = sb("eg", [RT, RN, E])
        gmx = sb("gmx", [RT, RN])
        gp = sb("gp", [RT, RN, E])
        gsum = sb("gsum", [RT, RN])
        gall = sb("gall", [RT, RN])
        ginv = sb("ginv", [RT, RN])
        gt = sb("gt", [RT, RN, E, E])
        eq = sb("eq", [RT, RN, E, E])
        rank = sb("rank", [RT, RN, E])
        c9 = sb("c9", [RT, RN, 9])
        c3 = sb("c3", [RT, RN, 3, E], bf16)
        cres = sb("cres", [RT, RN, E])
        cT3 = sb("cT3", [24, COLS], bf16)
        cT9 = sb("cT9", [128, COLS])
        HS = sb("HS", [128, COLS])
        HE = [sb(f"HE{i}", [128, COLS]) for i in range(4)]
        CW = [sb(f"CW{i}", [128, COLS]) for i in range(4)]
        GE = [sb(f"GE{i}", [128, COLS]) for i in range(4)]
        h2 = sb("h2", [128, COLS])
        OUTS = [sb(f"OUTS{p}", [RT, RN, 128]) for p in range(2)]

        bank = [ctx.enter_context(nc.psum_tensor(f"bank{i}", [128, 512], fp32)) for i in range(8)]

        bank3b = bank[3][:, :].bitcast(bf16)

        def cols(t):
            return bank[t][:, 0:COLS]

        const_in, zeroed, psum_zeroed, setup_psum, setup_mats, dve_consts = (
            sem(n) for n in ("const_in", "zeroed", "psum_zeroed", "setup_psum", "setup_mats", "dve_consts"))
        blk_in = sem("blk_in")
        ident_in, first_in = sem("ident_in"), sem("first_in")
        x_in = [[sem(f"x_in{p}{j}") for j in range(3)] for p in range(2)]
        gathered = [[sem(f"gathered{p}{j}") for j in range(3)] for p in range(2)]
        out_done = [sem(f"out_done{p}") for p in range(2)]
        tp_full = sem("tp_full")
        xt_ready, vt_ready = sem("xt_ready"), sem("vt_ready")
        off4_full, off4_ready, ot_full, ot_read, idx_ready = (
            sem(n) for n in ("off4_full", "off4_ready", "ot_full", "ot_read", "idx_ready"))
        val_ready, tok_full, h0_ready = (sem(n) for n in ("val_ready", "tok_full", "h0_ready"))
        hc_full, sq_ready, hc_ready, var_full, diag_ready, rstd_full, z_ready = (
            sem(n) for n in ("hc_full", "sq_ready", "hc_ready", "var_full", "diag_ready", "rstd_full", "z_ready"))
        hqk_full, y_full, y_ready, v_full, v_ready, add_ready, th_ready = (
            sem(n) for n in ("hqk_full", "y_full", "y_ready", "v_full", "v_ready", "add_ready", "th_ready"))
        s_full, sc_ready, exp_ready, p_ready, pt_full, pt_ready, av_full, h1_ready = (
            sem(n) for n in ("s_full", "sc_ready", "exp_ready", "p_ready", "pt_full",
                             "pt_ready", "av_full", "h1_ready"))
        gl_full, lg_ready, gexp_ready, c_ready, ct_full, ct_ready = (
            sem(n) for n in ("gl_full", "lg_ready", "gexp_ready", "c_ready", "ct_full", "ct_ready"))
        up_full, he_ready, cb_full, ge_ready, down_done, yacc_full, h2_ready, out_full, outs_ready = (
            sem(n) for n in ("up_full", "he_ready", "cb_full", "ge_ready", "down_done", "yacc_full", "h2_ready",
                             "out_full", "outs_ready"))
        cw_ready = sem("cw_ready")
        passed = sem("passed")
        dve_chain, act_chain = sem("dve_chain"), sem("act_chain")

        def groups_x(m, h):
            return 6 * h if isinstance(m, int) and m == 0 else 12 * (2 * m + h) - 6

        def groups_v(u):
            if isinstance(u, int) and u == UNITS - 1:
                return 12 * u + 6
            return 12 * u + 12

        def steps(eng, engine, pieces, chain=None, last=(UNITS - 4) // 2):
            def step(i, t):
                for name in (END_ORDER.get(t, ORDER) if isinstance(i, int) else ORDER)[engine]:
                    v = t + AHEAD[name[0]]
                    if not isinstance(i, int):
                        pieces[name](i + v // 2, v % 2)
                    elif 0 <= v < UNITS:
                        pieces[name](v // 2, v % 2)

            for s in (-1, 0):
                step(0, s)
            if chain:
                chain.mark()
            for s in (1, 2):
                step(0, s)
            per = chain.n - chain.at if chain else 0
            with eng.Fori(1, last) as i:
                if chain:
                    chain.loop(i, 1, per)
                for r in (1, 2):
                    step(i, r)
            if chain:
                chain.end(last - 1, per)
            for s in range(2 * last + 1, UNITS + 1):
                step(0, s)

        block = ctx.enter_context(nc.Block())

        @block.sync
        def _(sp):
            def load_x(m, h):
                u = 2 * m + h
                for j in range(3):
                    if not (isinstance(m, int) and m == 0):
                        sp.wait_ge(tp_full, groups_x(m - 1, h) + 2 * (j + 1))
                    src = x[bass.ds(NB * u, NB), W0[j] * K * C:(W0[j] + WT[j]) * K * C]
                    sp.dma_start(xt[h][0:NT[j], j, :],
                                 src.rearrange("b (w n) -> w b n", w=WT[j])).then_inc(x_in[h][j], 16)

            def next_x(m, h):
                m, h = m + (h + 1) // 2, (h + 1) % 2
                if not (isinstance(m, int) and 2 * m + h >= UNITS):
                    load_x(m, h)

            def store(m, h):
                u = 2 * m + h
                sp.wait_ge(outs_ready, u + 1)
                sp.dma_start(out[bass.ds(COLS * u, COLS), :].rearrange("(t r) d -> r t d", r=RT),
                             OUTS[h][:, :, :]).then_inc(out_done[h], 16)

            load_x(0, 0)
            load_x(0, 1)
            for name, _s in CONSTS[NFIRST:]:
                sp.dma_start(cs[name][:, :], consts[name]).then_inc(const_in, 16)
            sp.wait_ge(zeroed, 2)
            for b in range(NB):
                sp.dma_start(w2blk[H * b:H * b + H, b:b + 1], rows["w2col"]).then_inc(blk_in, 16)
            sp.dma_start(b2pad[0:9, :], rows["b2e"]).then_inc(blk_in, 16)
            load_x(1, 0)
            steps(sp, "sync", {"a0": next_x, "d9": store}, last=(UNITS - 4) // 2 - 1)
            for h in range(2):
                sp.wait_ge(out_done[h], 16 * UNITS // 2)

        @block.gpsimd
        def _(pool):
            pool.memset(w2blk[:, :], 0.0).then_inc(zeroed, 1)
            pool.memset(b2pad[:, :], 0.0).then_inc(zeroed, 1)
            pool.memset(w1pad[:, :, :, :], 0.0).then_inc(zeroed, 1)
            pool.memset(PT[:, :], 0.0).then_inc(zeroed, 1)
            pool.memset(V[:, :, :], 0.0).then_inc(zeroed, 1)
            pool.memset(cT9[:, :], 0.0).then_inc(zeroed, 1)
            pool.memset(c9[:, :, :], 1.0).then_inc(zeroed, 1)
            pool.memset(ones[:, :], 1.0).then_inc(zeroed, 1)
            pool.memset(mean1[:, :], 1.0 / D).then_inc(zeroed, 1)

            def gathers(m, h):
                u = 2 * m + h
                pool.wait_ge(idx_ready, u + 1)
                for j in range(3):
                    if not (isinstance(m, int) and m == 0):
                        pool.wait_ge(val_ready, 3 * u - 5 + j)
                    pool.sem_inc(passed, 1)
                    for k in range(K):
                        col = j * K + k
                        pool.indirect_dma_start(
                            out=G[h][0:NT[j], j, k, :], out_offset=None, in_=x.rearrange("b (l c) -> (b l) c", c=C),
                            in_offset=bass.IndirectOffsetOnAxis(ap=idx[h][0:NT[j], col:col + 1], axis=0),
                        ).then_inc(gathered[h][j], 16)

            gathers(0, 0)
            gathers(0, 1)
            with pool.Fori(1, UNITS // 2) as i:
                gathers(i, 0)
                gathers(i, 1)

        @block.scalar
        def _(act):
            chain = Chain(act, act_chain)
            act.dma_start(ident[:, :], consts["ident"]).then_inc(ident_in, 16)
            for name, _s in CONSTS[1:NFIRST]:
                act.dma_start(cs[name][:, :], consts[name]).then_inc(first_in, 16)

            def evacuate(first, n, dst, nrow, ready):
                act.wait_ge(tp_full, first + n + 1)
                act.activation(dst, bank[n % 2][:, 0:4 * nrow].rearrange("p (k t) -> p k t", k=4), ACT.Copy).then_inc(ready, 1)

            def turned_x(j):
                def piece(m, h):
                    if j == 0:
                        wait(act, off4_full, 2 * m + h)
                    for half in range(2):
                        evacuate(groups_x(m, h), 2 * j + half, XT[:, 4 * half:4 * half + 4, T0[j]:T0[j] + NT[j]], NT[j], xt_ready)
                return piece

            def turned_values(j):
                def piece(m, h):
                    u = 2 * m + h
                    if j == 0:
                        wait(act, tok_full, u)
                    for half in range(2):
                        evacuate(groups_v(u), 2 * j + half, VT[:, 4 * half:4 * half + 4, T0[j]:T0[j] + NT[j]], NT[j], vt_ready)
                return piece

            def offsets_out(m, h):
                u = 2 * m + h
                wait(act, ot_full, u)
                act.wait_ge(off4_full, u + 1)
                act.activation(off4[:, :], bank[0][:, 0:TOK], ACT.Copy).then_inc(off4_ready, 1)

            def squares(second):
                def piece(m, h):
                    act.wait_ge(hc_full, 2 * (2 * m + h) + second + 1)
                    act.activation(SQ[:, :], cols(5), ACT.Square).then_inc(sq_ready, 1)
                    act.activation(HC[:, :], cols(5), ACT.Copy).then_inc(hc_ready, 1)
                return piece

            def value_rows(u, half):
                act.wait_ge(v_full, 2 * u + half + 1)
                act.activation(V[0:S, 4 * half:4 * half + 4, :],
                               bank[6][0:S, :].rearrange("p (b n) -> p b n", b=4), ACT.Copy).then_inc(v_ready, 1)

            def hidden_tanh(u, half):
                act.wait_ge(add_ready, 2 * u + half + 1)
                k0, k1 = (0, KH) if half == 0 else (KH, S)
                act.activation(TH[:, k0:k1, :], TH[:, k0:k1, :], ACT.Tanh).then_inc(th_ready, 1)

            def m3(m, h):
                u = 2 * m + h
                act.wait_ge(y_full, u + 1)
                act.activation(Y[:, :, :].rearrange("p b s -> p (b s)"), cols(7), ACT.Copy).then_inc(y_ready, 1)
                value_rows(u, 0)

            def m4(m, h):
                u = 2 * m + h
                hidden_tanh(u, 0)
                value_rows(u, 1)

            def m5(m, h):
                hidden_tanh(2 * m + h, 1)

            def m6(m, h):
                act.wait_ge(sc_ready, 2 * m + h + 1)
                act.activation(SC[:, :, :], SC[:, :, :], ACT.Exp).then_inc(exp_ready, 1)

            def m7(m, h):
                act.wait_ge(pt_full, 2 * m + h + 1)
                act.activation(PT[0:S, :], bank[5][0:S, 0:COLS], ACT.Copy).then_inc(pt_ready, 1)

            def m12(m, h):
                act.wait_ge(lg_ready, 2 * m + h + 1)
                act.activation(eg[:, :, :], lg[:, :, :], ACT.Exp).then_inc(gexp_ready, 1)

            def gc(m, h):
                u = 2 * m + h
                act.wait_ge(ct_full, 2 * u + 1)
                act.activation(cT3[:, :], bank3b[0:24, 0:COLS], ACT.Copy).then_inc(ct_ready, 1)
                act.wait_ge(ct_full, 2 * u + 2)
                act.activation(cT9[0:9, :], bank[4][0:9, 0:COLS], ACT.Copy).then_inc(ct_ready, 1)

            def shared_hidden(m, h):
                u = 2 * m + h
                act.wait_ge(up_full, 9 * u + 1)
                wait(act, down_done, 9 * u - 8)
                act.activation(HS[:, :], cols(2), ACT.Relu, bias=cs["fb1"][:, E:E + 1]).then_inc(he_ready, 1)

            def hidden(e):
                def piece(m, h):
                    u = 2 * m + h
                    act.wait_ge(up_full, 9 * u + e + 2)
                    wait(act, ge_ready, 8 * u + e - 3)
                    act.activation(HE[e % 4][:, :], cols(2), ACT.Relu, bias=cs["fb1"][:, e:e + 1]).then_inc(he_ready, 1)
                return piece

            def weights(e):
                def piece(m, h):
                    u = 2 * m + h
                    act.wait_ge(cb_full, 8 * u + e + 1)
                    wait(act, ge_ready, 8 * u + e - 3)
                    act.activation(CW[e % 4][:, :], cols(3), ACT.Copy).then_inc(cw_ready, 1)
                return piece

            def d9(m, h):
                act.wait_ge(out_full, 2 * m + h + 1)
                if not (isinstance(m, int) and m == 0):
                    act.wait_ge(out_done[h], 16 * m)
                act.activation(OUTS[h][:, :, :], bank[2][0:RT, :].rearrange("p (t n) -> p t n", t=RN),
                               ACT.Copy).then_inc(outs_ready, 1)

            act.wait_ge(zeroed, 9)
            act.activation(tables[:, :], mean1[:, :], ACT.Copy)
            act.wait_ge(psum_zeroed, 2)
            for h in range(2):
                for j in range(3):
                    turned_x(j)(0, h)
                offsets_out(0, h)
            act.wait_ge(psum_zeroed, 8)
            act.wait_ge(setup_psum, 3)
            act.activation(scoreB[:, :], bank[5][:, 0:128], ACT.Copy, scale=float(D) ** -0.5).then_inc(setup_mats, 1)
            act.wait_ge(zeroed, 9)
            for qk in range(2):
                for par in range(2):
                    act.activation(w1pad[:, qk, par, H * par:H * par + H], bank[6 + qk][:, 0:H], ACT.Copy).then_inc(setup_mats, 1)
            pieces = {"m0": squares(0), "m3": m3, "m4": m4, "m5": m5, "m6": m6, "m7": m7, "m9": squares(1), "m12": m12,
                      "gc": gc, "fs": shared_hidden, "d9": d9, "a3": offsets_out}
            pieces.update({f"a{j}": turned_x(j) for j in range(3)})
            pieces.update({f"b{j}": turned_values(j) for j in range(3)})
            pieces.update({f"f{e}": hidden(e) for e in range(E)})
            pieces.update({f"g{e}": weights(e) for e in range(E)})
            steps(act, "scalar", pieces)

        @block.vector
        def _(dve):
            chain = Chain(dve, dve_chain)
            for b in range(8):
                dve.memset(bank[b][:, :], 0.0).then_inc(psum_zeroed, 1)
            dve.wait_ge(ident_in, 16)
            dve.wait_ge(first_in, 16 * (NFIRST - 1))
            dve.tensor_copy(identb[:, :], ident[:, :]).then_inc(dve_consts, 1)
            chain(dve.tensor_copy(rowb[:, :], cs["rowbase"][:, :]))
            dve.wait_ge(psum_zeroed, 8)

            def stage_a(m, h):
                u = 2 * m + h
                dve.wait_ge(ot_full, u + 1)
                dve.tensor_tensor(offs[:, :, :], bank[1][:, 0:96].rearrange("p (j o) -> p j o", o=32),
                                  cs["boff"][:, :].unsqueeze(1).broadcast_to([128, 3, 32]), ALU.add).then_inc(ot_read, 1)
                dve.wait_ge(ot_read, u + 1)
                chain(dve.tensor_tensor(px[:, :, :], offs[:, :, K:2 * K], base, ALU.add))
                chain(dve.scalar_tensor_tensor(nwy[:, :, :], offs[:, :, 0:K], -1.0, offs[:, :, 0:K], ALU.mult, ALU.max))
                chain(dve.tensor_scalar(rr[:, :, :], px[:, :, :], -0.5, 0.0, ALU.add, ALU.max))
                chain(dve.tensor_scalar(nwy[:, :, :], nwy[:, :, :], 1.0, 1.0, ALU.min, ALU.subtract))
                chain(dve.tensor_scalar(rr[:, :, :], rr[:, :, :], float(L - 2), ROUND, ALU.min, ALU.add))
                chain(dve.tensor_scalar(rr[:, :, :], rr[:, :, :], ROUND, None, ALU.subtract))
                dve.tensor_tensor(idx[h][:, :].rearrange("p (j k) -> p j k", k=K), rr[:, :, :],
                                  rowb[:, :].unsqueeze(2).broadcast_to([128, 3, K]), ALU.add).then_inc(idx_ready, 1)
                dve.wait_ge(idx_ready, u + 1)
                chain(dve.tensor_tensor(e01[:, :, :, 0], px[:, :, :], rr[:, :, :], ALU.subtract))
                chain(dve.tensor_scalar(e01[:, :, :, 1], e01[:, :, :, 0], 1.0, None, ALU.subtract))
                chain(dve.scalar_tensor_tensor(e01f, e01f, -1.0, e01f, ALU.mult, ALU.max))
                chain(dve.tensor_scalar(e01f, e01f, 1.0, 1.0, ALU.min, ALU.subtract))
                chain(dve.tensor_scalar(rowb[:, :], rowb[:, :], float(NB * L), None, ALU.add))
                chain(dve.tensor_tensor(aw[h][:, :, :, :], e01[:, :, :, :],
                                        nwy[:, :, :].unsqueeze(3).broadcast_to([128, 3, K, 2]), ALU.mult))

            def rstd(second):
                def piece(m, h):
                    dve.wait_ge(var_full, 2 * (2 * m + h) + second + 1)
                    chain(dve.tensor_scalar(var[:, :], bank[6][0:RT, COLS:COLS + RN], EPS, None, ALU.add))
                    chain(dve.tensor_scalar(ishift[:, :], var[:, :].bitcast(i32), 1, None, ALU.logical_shift_right))
                    chain(dve.tensor_scalar(ry[:, :].bitcast(i32), ishift[:, :], -1.0, float(0x5F3759DF), ALU.mult, ALU.add))
                    for _i in range(3):
                        chain(dve.scalar_tensor_tensor(nt_[:, :], ry[:, :], -0.5, ry[:, :], ALU.mult, ALU.mult))
                        chain(dve.tensor_tensor(nt_[:, :], nt_[:, :], var[:, :], ALU.mult))
                        chain(dve.scalar_tensor_tensor(ry[:, :], nt_[:, :], 1.5, ry[:, :], ALU.add, ALU.mult))
                    dve.tensor_tensor(diag[:, :, :], ident[0:RT, 0:RT].unsqueeze(1).broadcast_to([RT, RN, RT]),
                                      ry[:, :].unsqueeze(2).broadcast_to([RT, RN, RT]), ALU.mult).then_inc(diag_ready, 1)
                return piece

            def normalize(second):
                def piece(m, h):
                    n = 2 * (2 * m + h) + second
                    dve.wait_ge(rstd_full, n + 1)
                    dve.wait_ge(hc_ready, n + 1)
                    dve.tensor_tensor(Z2[h][:, :] if second else Zf, HC[:, :], cols(6), ALU.mult).then_inc(z_ready, 1)
                return piece

            def combine(j):
                def piece(m, h):
                    u = 2 * m + h
                    dve.wait_ge(gathered[h][j], 16 * K * (m + 1))
                    g = G[h][0:NT[j], j, :, :].rearrange("p k (s c) -> p (k s) c", s=2)
                    w = aw[h][0:NT[j], j, :, :].rearrange("p k s -> p (k s)").unsqueeze(2).broadcast_to([NT[j], 2 * K, C])
                    chain(dve.tensor_tensor(g, g, w, ALU.mult))
                    if not (isinstance(m, int) and u == 0):
                        dve.wait_ge(tp_full, groups_v(u - 1) + 2 * (j + 1))
                    g = G[h][0:NT[j], j, :, :]
                    dve.tensor_tensor(VAL[0:NT[j], j, :].rearrange("p (k c) -> p k c", c=C), g[:, :, 0:C],
                                      g[:, :, C:2 * C], ALU.add).then_inc(val_ready, 1)
                return piece

            def b3(m, h):
                dve.wait_ge(tok_full, 2 * m + h + 1)
                for j in range(3):
                    s0 = 1 + W0[j]
                    ins = dve.tensor_tensor(
                        h0[h][:, :, s0:s0 + WT[j]].rearrange("p b s -> p s b"),
                        bank[0][:, T0[j]:T0[j] + NT[j]].rearrange("p (w b) -> p w b", b=NB),
                        pe_b[:, s0:s0 + WT[j]].unsqueeze(2).broadcast_to([128, WT[j], NB]), ALU.add)
                ins.then_inc(h0_ready, 1)

            def m3(m, h):
                dve.wait_ge(hqk_full, 2 * m + h + 1)
                chain(dve.tensor_scalar(hq[:, :], bank[5][:, 0:S], cs["b1h"][:, 0:1], None, ALU.add))
                chain(dve.tensor_copy(hk[:, :], bank[5][:, S:2 * S]))
                pair_sums(0)

            def pair_sums(half):
                k0, k1 = (0, KH) if half == 0 else (KH, S)
                dve.tensor_tensor(TH[:, k0:k1, :], hq[:, :].unsqueeze(1).broadcast_to([128, k1 - k0, S]),
                                  hk[:, k0:k1].unsqueeze(2).broadcast_to([128, k1 - k0, S]), ALU.add).then_inc(add_ready, 1)

            def m4(m, h):
                pair_sums(1)

            def m6(m, h):
                dve.wait_ge(s_full, 2 * m + h + 1)
                sc = bank[6][0:S, 0:COLS].rearrange("p (b s) -> p b s", b=NB)
                chain(dve.reduce_max(smx[:, :], sc, AX.X))
                chain(dve.tensor_scalar(smx[:, :], smx[:, :], cs["b2col"][0:S, 0:1], None, ALU.add))
                dve.scalar_tensor_tensor(SC[:, :, :], sc, cs["b2col"][0:S, 0:1],
                                         smx[:, :].unsqueeze(2).broadcast_to([S, NB, S]), ALU.add,
                                         ALU.subtract).then_inc(sc_ready, 1)

            def m7(m, h):
                dve.wait_ge(exp_ready, 2 * m + h + 1)
                chain(dve.reduce_sum(ssum[:, :], SC[:, :, :], AX.X))
                chain(dve.reciprocal(sinv[:, :], ssum[:, :]))
                dve.tensor_tensor(PR[:, :, :], SC[:, :, :], sinv[:, :].unsqueeze(2).broadcast_to([S, NB, S]),
                                  ALU.mult).then_inc(p_ready, 1)

            def m8(m, h):
                dve.wait_ge(av_full, 2 * m + h + 1)
                dve.tensor_tensor(h1[h][:, :], cols(7), h0[h][:, :, :].rearrange("p b s -> p (b s)"), ALU.add).then_inc(h1_ready, 1)

            def m12(m, h):
                u = 2 * m + h
                dve.wait_ge(gl_full, u + 1)
                glv = bank[7][0:RT, 0:RN * E].rearrange("p (t e) -> p t e", e=E)
                chain(dve.reduce_max(gmx[:, :], glv, AX.X))
                dve.tensor_tensor(lg[:, :, :], glv, gmx[:, :].unsqueeze(2).broadcast_to([RT, RN, E]),
                                  ALU.subtract).then_inc(lg_ready, 1)

            def m13(m, h):
                other = lg[:, :, :].unsqueeze(2).broadcast_to([RT, RN, E, E])
                own = lg[:, :, :].unsqueeze(3).broadcast_to([RT, RN, E, E])
                dve.wait_ge(lg_ready, 2 * m + h + 1)
                chain(dve.tensor_tensor(gt[:, :, :, :], other, own, ALU.subtract))
                gtv = gt[:, :, :, :].rearrange("p t i j -> p t (i j)")
                eqv = eq[:, :, :, :].rearrange("p t i j -> p t (i j)")
                chain(dve.scalar_tensor_tensor(eqv, gtv, 0.0, cs["tri"][0:RT, :].unsqueeze(1).broadcast_to([RT, RN, E * E]),
                                               ALU.is_equal, ALU.mult))
                chain(dve.scalar_tensor_tensor(gtv, gtv, 0.0, eqv, ALU.is_gt, ALU.add))
                chain(dve.reduce_sum(rank[:, :, :], gt[:, :, :, :], AX.X))

            def m14(m, h):
                dve.wait_ge(gexp_ready, 2 * m + h + 1)
                chain(dve.scalar_tensor_tensor(gp[:, :, :], rank[:, :, :], 2.0, eg[:, :, :], ALU.is_lt, ALU.mult))
                chain(dve.reduce_sum(gall[:, :], eg[:, :, :], AX.X))
                chain(dve.reduce_sum(gsum[:, :], gp[:, :, :], AX.X))
                chain(dve.scalar_tensor_tensor(gsum[:, :], gall[:, :], 1e-20, gsum[:, :], ALU.mult, ALU.add))
                chain(dve.reciprocal(ginv[:, :], gsum[:, :]))
                chain(dve.tensor_tensor(c9[:, :, 0:E], gp[:, :, :], ginv[:, :].unsqueeze(2).broadcast_to([RT, RN, E]), ALU.mult))
                chain(dve.tensor_copy(c3[:, :, 0, :], c9[:, :, 0:E]))
                chain(dve.tensor_tensor(cres[:, :, :], c9[:, :, 0:E], c3[:, :, 0, :], ALU.subtract))
                chain(dve.tensor_copy(c3[:, :, 1, :], cres[:, :, :]))
                dve.tensor_tensor(c3[:, :, 2, :], cres[:, :, :], c3[:, :, 1, :], ALU.subtract).then_inc(c_ready, 1)

            def weighted(e):
                def piece(m, h):
                    u = 2 * m + h
                    dve.wait_ge(he_ready, 9 * u + e + 2)
                    dve.wait_ge(cw_ready, 8 * u + e + 1)
                    wait(dve, down_done, 9 * u + e - (2 if e >= 4 else 3))
                    dve.tensor_tensor(GE[e % 4][:, :], HE[e % 4][:, :], CW[e % 4][:, :], ALU.mult).then_inc(ge_ready, 1)
                return piece

            def d8(m, h):
                dve.wait_ge(yacc_full, 2 * m + h + 1)
                dve.tensor_tensor(h2[:, :], cols(4), h1[h][:, :], ALU.add).then_inc(h2_ready, 1)

            stage_a(0, 0)
            stage_a(0, 1)
            dve.wait_ge(const_in, 16 * (len(CONSTS) - NFIRST))
            dve.tensor_copy(selb[:, :, :].rearrange("p e n -> p (e n)"), cs["sel"][:, :]).then_inc(dve_consts, 1)
            dve.tensor_scalar(pe_b[:, :], cs["peT"][:, :], cs["bdef"][:, 0:1], None, ALU.add).then_inc(dve_consts, 1)
            dve.tensor_tensor(cls_pe[:, :], cs["cls"][:, :], cs["peT"][:, 0:1], ALU.add).then_inc(dve_consts, 1)
            dve.wait_ge(dve_consts, 4)
            for p in range(2):
                chain(dve.tensor_copy(h0[p][:, :, 0:1], cls_pe[:, :].unsqueeze(1).broadcast_to([128, NB, 1])))
            dve.wait_ge(zeroed, 9)
            pieces = {"m1": rstd(0), "m2": normalize(0), "m3": m3, "m4": m4, "m6": m6, "m7": m7, "m8": m8, "m10": rstd(1),
                      "m11": normalize(1), "m12": m12, "m13": m13, "m14": m14, "d8": d8, "b3": b3, "a4": stage_a}
            pieces.update({f"c{j}": combine(j) for j in range(3)})
            pieces.update({f"g{e}": weighted(e) for e in range(E)})
            steps(dve, "vector", pieces, chain)

        @block.tensor
        def _(pe):
            def turn(n, srcs, nrow):
                for i, src in enumerate(srcs):
                    mm = pe.transpose(bank[n % 2][:, i * nrow:(i + 1) * nrow], src, ident[0:nrow, 0:nrow])
                mm.then_inc(tp_full, 1)

            def four(t, j, half):
                return [t[0:NT[j], j, 128 * k:128 * k + 128] for k in range(4 * half, 4 * half + 4)]

            def turn_x(j):
                def piece(m, h):
                    u = 2 * m + h
                    pe.wait_ge(x_in[h][j], 16 * (m + 1))
                    for n in (2 * j, 2 * j + 1):
                        if n >= 2:
                            pe.wait_ge(xt_ready, 6 * u + n - 1)
                        elif n == 0 and not (isinstance(m, int) and m == 0):
                            pe.wait_ge(h0_ready, u - 1)
                        elif n == 1 and isinstance(m, int) and u == 1:
                            pe.wait_ge(ot_read, 1)
                        turn(n, four(xt[h], j, n % 2), NT[j])
                return piece

            def turn_values(j):
                def piece(m, h):
                    u = 2 * m + h
                    last = isinstance(m, int) and u == UNITS - 1
                    pe.wait_ge(val_ready, 3 * u + j + 1)
                    for n in (2 * j, 2 * j + 1):
                        if n >= 2:
                            pe.wait_ge(vt_ready, 6 * u + n - 1)
                        elif n == 0 and last:
                            pe.wait_ge(h0_ready, u)
                        elif n == 1 and not last:
                            pe.wait_ge(ot_read, u + 2)
                        turn(n, four(VAL, j, n % 2), NT[j])
                return piece

            def b3(m, h):
                pe.wait_ge(vt_ready, 6 * (2 * m + h + 1))
                for kp in range(KP):
                    mm = pe.matmul(bank[0][:, 0:TOK], wdef[:, kp, :], VT[:, kp, :], start=(kp == 0), stop=(kp == KP - 1))
                mm.then_inc(tok_full, 1)

            def a3(m, h):
                pe.wait_ge(xt_ready, 6 * (2 * m + h + 1))
                for r in range(2):
                    for g in range(4):
                        kp = 4 * r + g
                        mm = pe.matmul(bank[0][32 * g:32 * g + 32, 0:TOK], wof[:, kp, :], XT[:, kp, :],
                                       start=(r == 0), stop=(r == 1), skip_group_check=True)
                mm.then_inc(off4_full, 1)

            def a4(m, h):
                pe.wait_ge(off4_ready, 2 * m + h + 1)
                for j in range(3):
                    mm = pe.matmul(bank[1][0:NT[j], 32 * j:32 * j + 32], off4[:, T0[j]:T0[j] + NT[j]], cs["stk"][:, :],
                                   start=True, stop=True)
                mm.then_inc(ot_full, 1)

            def centered(second):
                def piece(m, h):
                    if second:
                        pe.wait_ge(h1_ready, 2 * m + h + 1)
                        src = h1[h][:, :]
                    else:
                        pe.wait_ge(h0_ready, 2 * m + h + 1)
                        src = h0[h][:, :, :].rearrange("p b s -> p (b s)")
                    pe.matmul(cols(5), center[:, :], src, start=True, stop=True).then_inc(hc_full, 1)
                return piece

            def variance(second):
                def piece(m, h):
                    pe.wait_ge(sq_ready, 2 * (2 * m + h) + second + 1)
                    for t in range(RN):
                        mm = pe.matmul(bank[6][0:RT, COLS + t:COLS + t + 1], SQ[:, RT * t:RT * t + RT], mean1[:, :],
                                       start=True, stop=True)
                    mm.then_inc(var_full, 1)
                return piece

            def spread_rstd(second):
                def piece(m, h):
                    pe.wait_ge(diag_ready, 2 * (2 * m + h) + second + 1)
                    pe.matmul(cols(6), ones[0:RT, :], diag[:, :, :].rearrange("p t r -> p (t r)"),
                              start=True, stop=True).then_inc(rstd_full, 1)
                return piece

            def values(u, half):
                for b in range(4 * half, 4 * half + 4):
                    mm = pe.matmul(bank[6][0:S, 128 * (b % 4):128 * (b % 4) + 128], Z[:, b, :], cs["wvT"][:, :],
                                   start=True, stop=True)
                mm.then_inc(v_full, 1)

            def m3(m, h):
                u = 2 * m + h
                pe.wait_ge(z_ready, 2 * u + 1)
                for qk in range(2):
                    for par in range(2):
                        for g in range(4):
                            mm = pe.matmul(bank[5][32 * g:32 * g + 32, qk * S:qk * S + S], w1pad[:, qk, par, :],
                                           Z[:, 2 * g + par, :], start=(par == 0), stop=(par == 1), skip_group_check=True)
                mm.then_inc(hqk_full, 1)
                pe.matmul(cols(7), scoreB[:, :], Zf, start=True, stop=True).then_inc(y_full, 1)
                values(u, 0)

            def m4(m, h):
                u = 2 * m + h
                pe.wait_ge(v_ready, 2 * u + 1)
                values(u, 1)

            def m5(m, h):
                u = 2 * m + h
                pe.wait_ge(y_ready, u + 1)
                pe.wait_ge(v_ready, 2 * u + 2)
                for b in range(NB):
                    mm = pe.matmul(bank[6][0:S, S * b:S * b + S], Y[:, b, :], Z[:, b, :], start=(b == 0), stop=True,
                              skip_group_check=True)
                for k in range(S):
                    if k in (0, KH):
                        pe.wait_ge(th_ready, 2 * u + (1 if k == 0 else 2))
                    mm = pe.matmul(bank[6][0:S, k:k + S * (NB - 1) + 1:S], TH[:, k, :], w2blk[:, :],
                                   start=False, stop=True, skip_group_check=True)
                mm.then_inc(s_full, 1)

            def m7(m, h):
                pe.wait_ge(p_ready, 2 * m + h + 1)
                pe.sem_inc(passed, 1)
                for b in range(NB):
                    mm = pe.transpose(bank[5][0:S, S * b:S * b + S], PR[:, b, :], ident[0:S, 0:S])
                mm.then_inc(pt_full, 1)

            def m8(m, h):
                pe.wait_ge(pt_ready, 2 * m + h + 1)
                for b in range(NB):
                    mm = pe.matmul(bank[7][:, S * b:S * b + S], V[:, b, :], PT[:, S * b:S * b + S], start=True, stop=True)
                mm.then_inc(av_full, 1)

            def m12(m, h):
                u = 2 * m + h
                pe.wait_ge(z_ready, 2 * u + 2)
                for t in range(RN):
                    mm = pe.matmul(bank[7][0:RT, E * t:E * t + E], Z2[h][:, RT * t:RT * t + RT], cs["gwT"][:, :],
                                   start=True, stop=True)
                mm.then_inc(gl_full, 1)

            def gc(m, h):
                u = 2 * m + h
                pe.wait_ge(c_ready, u + 1)
                wait(pe, cw_ready, 8 * u)
                for t in range(RN):
                    mm = pe.transpose(bank3b[0:24, RT * t:RT * t + RT], c3[:, t, :, :].rearrange("p a e -> p (a e)"),
                                      identb[0:RT, 0:RT])
                mm.then_inc(ct_full, 1)
                wait(pe, h2_ready, u)
                for t in range(RN):
                    mm = pe.transpose(bank[4][0:9, RT * t:RT * t + RT], c9[:, t, :], ident[0:RT, 0:RT])
                mm.then_inc(ct_full, 1)

            def up(e):
                def piece(m, h):
                    u = 2 * m + h
                    if e == E:
                        wait(pe, outs_ready, u)
                    else:
                        pe.wait_ge(he_ready, 9 * u + e + 1)
                    pe.matmul(cols(2), w1e[:, e, :], Z2[h][:, :], start=True, stop=True).then_inc(up_full, 1)
                return piece

            def spread_weights(e):
                def piece(m, h):
                    u = 2 * m + h
                    if e == 0:
                        pe.wait_ge(ct_ready, 2 * u + 1)
                    else:
                        pe.wait_ge(cw_ready, 8 * u + e)
                    pe.matmul(cols(3), selb[:, e, :], cT3[:, :], start=True, stop=True).then_inc(cb_full, 1)
                return piece

            def down(e):
                def piece(m, h):
                    u = 2 * m + h
                    if e == E:
                        pe.wait_ge(he_ready, 9 * u + 1)
                        pe.wait_ge(ct_ready, 2 * u + 2)
                    else:
                        pe.wait_ge(ge_ready, 8 * u + e + 1)
                    pe.matmul(cols(4), w2e[:, e, :], HS[:, :] if e == E else GE[e % 4][:, :],
                              start=(e == E), stop=False).then_inc(down_done, 1)
                return piece

            def d8(m, h):
                pe.matmul(cols(4), b2pad[:, :], cT9[:, :], start=False, stop=True).then_inc(yacc_full, 1)

            def d9(m, h):
                pe.wait_ge(h2_ready, 2 * m + h + 1)
                for t in range(RN):
                    mm = pe.transpose(bank[2][0:RT, 128 * t:128 * t + 128], h2[:, RT * t:RT * t + RT], ident[:, :])
                mm.then_inc(out_full, 1)

            pe.wait_ge(ident_in, 16)
            pe.wait_ge(psum_zeroed, 2)
            for h in range(2):
                for j in range(3):
                    turn_x(j)(0, h)
                pe.wait_ge(first_in, 16 * (NFIRST - 1))
                a3(0, h)
                a4(0, h)
            pe.wait_ge(blk_in, 16 * (NB + 1))
            pe.wait_ge(const_in, 16 * (len(CONSTS) - NFIRST))
            pe.wait_ge(zeroed, 9)
            pe.wait_ge(psum_zeroed, 8)
            pe.wait_ge(dve_consts, 4)
            pe.matmul(bank[5][:, 0:128], cs["wq"][:, :], cs["wk"][:, :], start=True, stop=True).then_inc(setup_psum, 1)
            pe.matmul(bank[6][:, 0:H], cs["wq"][:, :], cs["w1qT"][:, :], start=True, stop=True).then_inc(setup_psum, 1)
            pe.matmul(bank[7][:, 0:H], cs["wk"][:, :], cs["w1kT"][:, :], start=True, stop=True).then_inc(setup_psum, 1)
            pe.wait_ge(setup_mats, 5)
            pieces = {"m0": centered(0), "m1": variance(0), "m2": spread_rstd(0), "m3": m3, "m4": m4, "m5": m5, "m7": m7,
                      "m8": m8, "m9": centered(1), "m10": variance(1), "m11": spread_rstd(1), "m12": m12,
                      "gc": gc, "fs": up(E), "ds": down(E), "d8": d8, "d9": d9, "b3": b3, "a3": a3, "a4": a4}
            pieces.update({f"a{j}": turn_x(j) for j in range(3)})
            pieces.update({f"b{j}": turn_values(j) for j in range(3)})
            pieces.update({f"f{e}": up(e) for e in range(E)})
            pieces.update({f"g{e}": spread_weights(e) for e in range(E)})
            pieces.update({f"d{e}": down(e) for e in range(E)})
            steps(pe, "tensor", pieces)


def kernel(**inputs):
    import numpy as np
    import concourse.bacc as bacc
    from concourse.bass_utils import run_bass_kernel_spmd

    f = np.float32
    a = {n: np.asarray(v) for n, v in inputs.items()}
    p = np.arange(128)

    def taps(w):
        o = w.shape[0]
        return w.transpose(2, 1, 0).reshape(KP, 2, C, o).transpose(1, 2, 0, 3).reshape(128, KP * o)

    pos = np.arange(S, dtype=f)[:, None]
    div = np.exp(np.arange(0, D, 2, dtype=f) * f(-np.log(10000.0) / D))
    pe = np.zeros((S, D), f)
    pe[:, 0::2] = np.sin(pos * div)
    pe[:, 1::2] = np.cos(pos * div)
    base = np.stack([(W0[j] + p // NB)[:, None] * K + np.arange(K)[None, :] for j in range(3)], 1).astype(f)
    sel = np.zeros((24, E, 128), f)
    for r in range(24):
        sel[r, r % E] = 1
    dydx = np.r_[np.arange(0, 32, 2), np.arange(1, 32, 2)]
    boff = a["L0_tok_b_off"][dydx]
    W1 = a["L0_attn_W1"]
    host = {
        "ident": np.eye(128, dtype=f), "wof": taps(a["L0_tok_w_off"][dydx]), "stk": np.tile(np.eye(32, dtype=f), (4, 1)),
        "boff": np.broadcast_to(boff, (128, 32)), "base": base.reshape(128, 48),
        "rowbase": np.repeat((p % NB * L)[:, None], 3, 1).astype(f), "wdef": taps(a["L0_tok_w_def"]),
        "bdef": a["L0_tok_b_def"][:, None], "cls": a["L0_tok_cls_token"].reshape(128, 1), "peT": pe.T,
        "center": (np.eye(128) - 1.0 / D).astype(f), "wq": a["L0_attn_Wq"], "wk": a["L0_attn_Wk"], "wvT": a["L0_attn_Wv"].T,
        "w1qT": W1[:, :D].T, "w1kT": W1[:, D:].T, "b1h": np.tile(a["L0_attn_b1"], NB)[:, None],
        "gwT": a["L0_ffn_gate_w"].T, "tri": np.broadcast_to(np.tril(np.ones((E, E), f), -1).reshape(1, 64), (128, 64)),
        "w1e": np.concatenate([a["L0_ffn_w1"], a["L0_ffn_sw1"][None]]).transpose(1, 0, 2).reshape(128, 9 * 128),
        "w2e": np.concatenate([a["L0_ffn_w2"], a["L0_ffn_sw2"][None]]).transpose(1, 0, 2).reshape(128, 9 * 128),
        "fb1": np.concatenate([a["L0_ffn_b1"], a["L0_ffn_sb1"][None]]).T, "sel": sel.reshape(24, E * 128),
        "b2col": np.broadcast_to(a["L0_attn_b2"], (128, 1)),
        "w2col": a["L0_attn_W2"].T, "b2e": np.concatenate([a["L0_ffn_b2"], a["L0_ffn_sb2"][None]]),
        "x": a["x"].reshape(B, L * C),
    }
    nc = bacc.Bacc("TRN2", target_bir_lowering=False, num_devices=1)
    arrays, aps = {}, {}
    for name, v in host.items():
        v = np.ascontiguousarray(v)
        arrays[f"in_{name}"] = v
        aps[name] = nc.dram_tensor(f"in_{name}", v.shape, mybir.dt.from_np(v.dtype), kind="ExternalInput").ap()
    out = nc.dram_tensor("out_0", (B * S, D), mybir.dt.float32, kind="ExternalOutput").ap()
    audio_tower(nc, aps["x"], aps, aps, out)
    r = run_bass_kernel_spmd(nc, [arrays], core_ids=[0])
    return r.results[0]["out_0"].reshape(B, S, D)
```
